# Optimizing a Trainium2 kernel written in Bass

```python
import numpy as np
import jax
import jax.numpy as jnp

def _softmax(x, axis=-1):
    return jax.nn.softmax(x, axis=axis)

def _gelu(x):
    return jax.nn.gelu(x, approximate=True)

def _silu(x):
    return jax.nn.silu(x)

def _sigmoid(x):
    return jax.nn.sigmoid(x)

def _layernorm(x, axis=-1, eps=1e-05):
    m = jnp.mean(x, axis=axis, keepdims=True)
    v = jnp.var(x, axis=axis, keepdims=True)
    return (x - m) / jnp.sqrt(v + eps)

def _scatter_add(tgt, idx, src, axis=0):
    return tgt.at[idx].add(src)

def _segment_sum(src, seg, n):
    return jax.ops.segment_sum(src, seg, n)
kernel_name = 'mk_seq_preln_d1_jaxref_r8_647397'

def setup_inputs(seed: int=0):
    np.random.seed(seed)
    _w = jnp.asarray

    def _L0_attn_setup():
        import jax, jax.numpy as jnp
        import numpy as np
        D_MODEL = 128
        EXPAND = 2
        D_INNER = EXPAND * D_MODEL
        D_HEAD = 64
        N_HEADS = D_INNER // D_HEAD
        D_STATE = 128
        D_CONV = 4
        PARAM_DIM = 1
        BC_DIM = N_HEADS * 4 * D_STATE
        IN_DIM = 2 * D_INNER + N_HEADS * PARAM_DIM + BC_DIM
        DT_MIN, DT_MAX = (0.0001, 0.1)
        THETA_BOUND = float(np.pi)
        K_MAX = 0.5
        EPS = 1e-08

        def _l2norm(t):
            return t / jnp.sqrt(jnp.sum(t * t, axis=-1, keepdims=True) + EPS)
        key = jax.random.key(seed)
        ks = jax.random.split(key, 9)
        x = jax.random.normal(ks[0], (2, 256, D_MODEL), jnp.float32)
        W_in = jax.random.normal(ks[1], (IN_DIM, D_MODEL), jnp.float32) / np.sqrt(D_MODEL)
        dw_weight = jax.random.normal(ks[2], (D_INNER, D_CONV), jnp.float32) / np.sqrt(D_CONV)
        dw_bias = jax.random.uniform(ks[3], (D_INNER,), jnp.float32, -0.5, 0.5)
        W_out = jax.random.normal(ks[4], (D_MODEL, D_INNER), jnp.float32) / np.sqrt(D_INNER)
        skip = jnp.ones((D_INNER,), jnp.float32)
        dt_bias = jax.random.normal(ks[5], (N_HEADS,), jnp.float32) * 0.5
        theta_raw = jax.random.normal(ks[6], (N_HEADS, D_STATE), jnp.float32)
        k_raw = jax.random.normal(ks[7], (N_HEADS, D_STATE), jnp.float32)
        return dict(x=x, W_in=W_in, dw_weight=dw_weight, dw_bias=dw_bias, W_out=W_out, skip=skip, dt_bias=dt_bias, theta_raw=theta_raw, k_raw=k_raw)
    _L0_attn_in = _L0_attn_setup()

    def _L0_ffn_setup():
        import jax, jax.numpy as jnp
        import numpy as np
        D = 128
        H = 256
        E = 8
        TOP_K = 2
        N_SHARED = 1
        B, S = (2, 128)
        key = jax.random.key(seed)
        ks = jax.random.split(key, 12)
        sc = 0.02
        return {'hidden': jax.random.normal(ks[0], (B, S, D), jnp.float32), 'router_w': jax.random.normal(ks[1], (D, E), jnp.float32) * sc, 'router_b': jnp.zeros((E,), jnp.float32), 'sw1': jax.random.normal(ks[2], (D, H), jnp.float32) * sc, 'sb1': jnp.zeros((H,), jnp.float32), 'sw2': jax.random.normal(ks[3], (H, D), jnp.float32) * sc, 'sb2': jnp.zeros((D,), jnp.float32), 'rw1': jax.random.normal(ks[4], (E, D, H), jnp.float32) * sc, 'rb1': jnp.zeros((E, H), jnp.float32), 'rw2': jax.random.normal(ks[5], (E, H, D), jnp.float32) * sc, 'rb2': jnp.zeros((E, D), jnp.float32)}
    _L0_ffn_in = _L0_ffn_setup()
    _d = {'L0_attn_x': _L0_attn_in['x'], 'L0_attn_W_in': _L0_attn_in['W_in'], 'L0_attn_dw_weight': _L0_attn_in['dw_weight'], 'L0_attn_dw_bias': _L0_attn_in['dw_bias'], 'L0_attn_W_out': _L0_attn_in['W_out'], 'L0_attn_skip': _L0_attn_in['skip'], 'L0_attn_dt_bias': _L0_attn_in['dt_bias'], 'L0_attn_theta_raw': _L0_attn_in['theta_raw'], 'L0_attn_k_raw': _L0_attn_in['k_raw'], 'L0_ffn_router_w': _L0_ffn_in['router_w'], 'L0_ffn_router_b': _L0_ffn_in['router_b'], 'L0_ffn_sw1': _L0_ffn_in['sw1'], 'L0_ffn_sb1': _L0_ffn_in['sb1'], 'L0_ffn_sw2': _L0_ffn_in['sw2'], 'L0_ffn_sb2': _L0_ffn_in['sb2'], 'L0_ffn_rw1': _L0_ffn_in['rw1'], 'L0_ffn_rb1': _L0_ffn_in['rb1'], 'L0_ffn_rw2': _L0_ffn_in['rw2'], 'L0_ffn_rb2': _L0_ffn_in['rb2']}
    _x0 = _d['L0_attn_x']
    _d['L0_attn_x'] = jax.random.normal(jax.random.fold_in(jax.random.key(seed), 1), (1, 2048, 128), dtype=_x0.dtype)
    del _x0
    return _d

def reference(L0_attn_x, L0_attn_W_in, L0_attn_dw_weight, L0_attn_dw_bias, L0_attn_W_out, L0_attn_skip, L0_attn_dt_bias, L0_attn_theta_raw, L0_attn_k_raw, L0_ffn_router_w, L0_ffn_router_b, L0_ffn_sw1, L0_ffn_sb1, L0_ffn_sw2, L0_ffn_sb2, L0_ffn_rw1, L0_ffn_rb1, L0_ffn_rw2, L0_ffn_rb2):

    def _L0_attn_ref(x, W_in, dw_weight, dw_bias, W_out, skip, dt_bias, theta_raw, k_raw):
        import jax, jax.numpy as jnp
        import numpy as np
        D_MODEL = 128
        EXPAND = 2
        D_INNER = EXPAND * D_MODEL
        D_HEAD = 64
        N_HEADS = D_INNER // D_HEAD
        D_STATE = 128
        D_CONV = 4
        PARAM_DIM = 1
        BC_DIM = N_HEADS * 4 * D_STATE
        IN_DIM = 2 * D_INNER + N_HEADS * PARAM_DIM + BC_DIM
        DT_MIN, DT_MAX = (0.0001, 0.1)
        THETA_BOUND = float(np.pi)
        K_MAX = 0.5
        EPS = 1e-08

        def _l2norm(t):
            return t / jnp.sqrt(jnp.sum(t * t, axis=-1, keepdims=True) + EPS)
        B, L, _ = x.shape
        proj = x @ W_in.T
        z, xc, dt_raw, bc = jnp.split(proj, [D_INNER, 2 * D_INNER, 2 * D_INNER + N_HEADS], axis=-1)
        xc = jnp.pad(xc.transpose(0, 2, 1), ((0, 0), (0, 0), (D_CONV - 1, 0)))
        xc = jax.lax.conv_general_dilated(xc, dw_weight[:, None, :], (1,), 'VALID', feature_group_count=D_INNER)
        u = jax.nn.silu(xc + dw_bias[None, :, None]).transpose(0, 2, 1)
        u = u.reshape(B, L, N_HEADS, D_HEAD)
        dt = jnp.clip(jax.nn.softplus(dt_raw + dt_bias), DT_MIN, DT_MAX)
        bc = bc.reshape(B, L, N_HEADS, 2, 2 * D_STATE)
        Bm = _l2norm(bc[..., 0, :])
        Cm = _l2norm(bc[..., 1, :])
        By, Bv = (Bm[..., :D_STATE], Bm[..., D_STATE:])
        Cy, Cv = (Cm[..., :D_STATE], Cm[..., D_STATE:])
        theta = THETA_BOUND * jax.nn.sigmoid(theta_raw)
        A = theta * theta
        kdamp = K_MAX * jax.nn.sigmoid(k_raw)

        def step(carry, inp):
            y, v = carry
            u_t, dt_t, By_t, Bv_t, Cy_t, Cv_t = inp
            dt4 = dt_t[:, :, None, None]
            denom = 1.0 + dt_t[:, :, None] * kdamp + dt_t[:, :, None] ** 2 * A
            v = (v - dt4 * A[None, :, None, :] * y + dt4 * u_t[..., None] * Bv_t[:, :, None, :]) / denom[:, :, None, :]
            y = y + dt4 * v + dt4 * u_t[..., None] * By_t[:, :, None, :]
            o = jnp.einsum('bhpn,bhn->bhp', y, Cy_t) + jnp.einsum('bhpn,bhn->bhp', v, Cv_t)
            return ((y, v), o)
        init = (jnp.zeros((B, N_HEADS, D_HEAD, D_STATE), x.dtype), jnp.zeros((B, N_HEADS, D_HEAD, D_STATE), x.dtype))
        xs = (u.transpose(1, 0, 2, 3), dt.transpose(1, 0, 2), By.transpose(1, 0, 2, 3), Bv.transpose(1, 0, 2, 3), Cy.transpose(1, 0, 2, 3), Cv.transpose(1, 0, 2, 3))
        _, o = jax.lax.scan(step, init, xs)
        o = o.transpose(1, 0, 2, 3).reshape(B, L, D_INNER)
        y_inner = o + skip * u.reshape(B, L, D_INNER)
        out = y_inner * jax.nn.silu(z) @ W_out.T
        return out

    def _L0_ffn_ref(hidden, router_w, router_b, sw1, sb1, sw2, sb2, rw1, rb1, rw2, rb2):
        import jax, jax.numpy as jnp
        import numpy as np
        D = 128
        H = 256
        E = 8
        TOP_K = 2
        N_SHARED = 1
        B, S = (2, 128)
        b, s, d = hidden.shape
        T = b * s
        flat = hidden.reshape(T, d)
        router_logits = flat @ router_w + router_b
        router_probs = jax.nn.softmax(router_logits, axis=-1)
        topk_probs, topk_idx = jax.lax.top_k(router_probs, TOP_K)
        weights = jnp.zeros_like(router_probs).at[jnp.arange(T)[:, None], topk_idx].add(topk_probs)
        sh = jax.nn.gelu(flat @ sw1 + sb1, approximate=False)
        shared_out = (sh @ sw2 + sb2) / N_SHARED
        h1 = jax.nn.gelu(jnp.einsum('td,edh->teh', flat, rw1) + rb1[None], approximate=False)
        expert_out = jnp.einsum('teh,ehd->ted', h1, rw2) + rb2[None]
        mixed = jnp.einsum('ted,te->td', expert_out, weights)
        return (shared_out + mixed).reshape(b, s, d)
    x = L0_attn_x
    x = x + _L0_attn_ref(_layernorm(x, axis=-1), L0_attn_W_in, L0_attn_dw_weight, L0_attn_dw_bias, L0_attn_W_out, L0_attn_skip, L0_attn_dt_bias, L0_attn_theta_raw, L0_attn_k_raw)
    x = x + _L0_ffn_ref(_layernorm(x, axis=-1), L0_ffn_router_w, L0_ffn_router_b, L0_ffn_sw1, L0_ffn_sb1, L0_ffn_sw2, L0_ffn_sb2, L0_ffn_rw1, L0_ffn_rb1, L0_ffn_rw2, L0_ffn_rb2)
    return x

_drawn_inputs = setup_inputs


def setup_inputs(seed=0):
    import zlib

    import numpy as np

    out = dict(_drawn_inputs(seed))
    spreads = {'L0_attn_skip': (1.0, 0.2),
     'L0_ffn_router_b': (0.0, 0.678),
     'L0_ffn_sb1': (0.0, 0.556),
     'L0_ffn_sb2': (0.0, 0.1),
     'L0_ffn_rb1': (0.0, 0.8),
     'L0_ffn_rb2': (0.0, 0.375)}
    factors = {'L0_attn_dt_bias': 8.0,
     'L0_attn_theta_raw': 4.536,
     'L0_attn_k_raw': 8.0,
     'L0_ffn_router_w': 2.856,
     'L0_ffn_rw1': 7.074,
     'L0_ffn_rw2': 6.306,
     'L0_ffn_sw1': 3.096}
    for name, (base, spread) in spreads.items():
        noise = np.random.default_rng([zlib.crc32(name.encode()), seed]).standard_normal(out[name].shape)
        drawn = base * np.exp(spread * noise) if base else spread * noise
        out[name] = jnp.asarray(drawn.astype(out[name].dtype))
    for name, factor in factors.items():
        out[name] = (out[name] * factor).astype(out[name].dtype)
    return out
```

```python
from contextlib import ExitStack

import concourse.bass as bass
from concourse import mybir

F32 = mybir.dt.float32
ALU = mybir.AluOpType
ACT = mybir.ActivationFunctionType
AX = mybir.AxisListType

T, DM = 2048, 128
NH, HD, NS = 4, 64, 128
DI = NH * HD
TAPS = 4
NE, NX, HF = 8, 9, 256
TS = 128
GT = 4
NT, NG = T // TS, T // (TS * GT)
KP = GT * NH
GC = GT * TS
SL = TS + 1
MID = TS // 2
PC = KP * SL
DT_MIN, DT_MAX = 1e-4, 0.1
E_MAX = 0.11
PI = 3.141592653589793
K_MAX = 0.5
EPS_LN, EPS_L2 = 1e-5, 1e-8
HALO = TAPS - 1
COL_Z, COL_U, COL_DT, COL_BC = 0, DI, 2 * DI, 2 * DI + NH
STEPS_PER_EXPERT = 7
STEP_OPS = 8 * MID + 1


def view(t, offset, *dims):
    full = t[:]
    return bass.AP(tensor=full.tensor, offset=full.offset + offset,
                   ap=[list(full.ap[0])] + [[s, n] for s, n in dims])


def build(nc, x, w_inT, dw_wT, dw_b, w_outT, skip, dt_bias, theta_rawT, k_rawT,
          router_w, router_b, sw1, sb1T, sw2, sb2, rw1, rb1T, rw2, rb2, out):
    ctx = ExitStack()
    with ctx:
        def sb(name, *shape, dtype=F32):
            return ctx.enter_context(nc.sbuf_tensor(name, list(shape), dtype))

        def sem(name):
            return ctx.enter_context(nc.semaphore(name))

        winT = sb("winT", DM, 2 * DI + NH + 4 * NH * NS)
        taps = sb("taps", DM, TAPS, DI)
        biasu = sb("biasu", 1, DI)
        woT = sb("woT", 128, 2, DM)
        skipb = sb("skipb", 128, DI)
        dtbb = sb("dtbb", 128, NH)
        theta = sb("theta", NS, NH)
        avec = sb("avec", NS, NH)
        kvec = sb("kvec", NS, NH)
        sgt = sb("sgt", NS, 4 * NH)
        rw = sb("rw", DM, NE)
        rb = sb("rb", 1, NE)
        w1 = sb("w1", DM, NX, HF)
        b1 = sb("b1", 128, NX, 2)
        w2 = sb("w2", 128, NX, 2, DM)
        b2 = sb("b2", NX, DM)
        ident = sb("ident", 128, 128)
        causal = sb("causal", 128, 128)
        before = sb("before", 128, NE, NE)
        ones = sb("ones", 128, 1)
        onesrow = sb("onesrow", 1, 128)
        eps_l2 = sb("eps_l2", 128, 1)
        mhalf = sb("mhalf", 128, 8)
        xr = [sb(f"xr{i}", 128, GT, DM) for i in range(3)]
        xn = sb("xn", 128, GT, DM)
        xnT = sb("xnT", DM, HALO + GC)
        stats = sb("stats", 128, GT, 6)
        mv = sb("mv", 128, GT, 2)
        rstd = sb("rstd", 128, GT)
        lraw = sb("lraw", 128, KP)
        lx = sb("lx", 128, KP)
        le = sb("le", 128, KP)
        lp = [sb(f"lp{i}", 128, KP) for i in range(2)]
        dtt = sb("dtt", 128, KP)
        dtr = sb("dtr", KP, TS)
        sqn = sb("sqn", NS, GT, TS)
        lden = sb("lden", NS, PC)
        de = sb("de", NS, 2 * PC)
        ab = sb("ab", NS, 2 * PC)
        DTN, LCS = 1, PC
        us = sb("us", 128, GT, DI)
        su = [sb(f"su{i}", 128, DI) for i in range(2)]
        sz = sb("sz", 128, GT, DI)
        pr = sb("pr", NS, 4 * PC)
        ta = [sb(f"ta{i}", NS, 2 * KP) for i in range(2)]
        tb = [sb(f"tb{i}", NS, 2 * KP) for i in range(2)]
        yc = [sb(f"yc{i}", NS, 4, TS) for i in range(2)]
        sq = [sb(f"sq{i}", NS, 4, TS) for i in range(2)]
        vc = [sb(f"vc{i}", NS, 2, TS) for i in range(2)]
        mm = [sb(f"mm{i}", NS, 4, 2, TS) for i in range(2)]
        wt = [sb(f"wt{i}", NS, 2, TS) for i in range(8)]
        vt = [sb(f"vt{i}", NS, 2, TS) for i in range(2)]
        vts = [sb(f"vts{i}", TS, 2, NS) for i in range(8)]
        gts = [sb(f"gts{i}", TS, TS) for i in range(8)]
        nrm = sb("nrm", 128, 8)
        rn = [sb(f"rn{i}", 128, 8) for i in range(2)]
        du = sb("du", 128, NH)
        ub = [sb(f"ub{i}", 128, DI) for i in range(2)]
        xi = [sb(f"xi{i}", NS, 2, DI) for i in range(2)]
        zz = sb("zz", NS, 2, DI)
        x1 = sb("x1", NS, 2, DI)
        x2 = sb("x2", NS, 2, DI)
        edge = sb("edge", NS, 4, NH + KP)
        ew = sb("ew", NS, 2, KP)
        tra = sb("tra", NS, 4, 2, KP)
        tr = sb("tr", NS, 2, 2, KP)
        y1 = [sb(f"y1{i}", 128, DI) for i in range(2)]
        y2 = sb("y2", 128, DI)
        y3 = sb("y3", 128, DI)
        yT = sb("yT", 128, 2, TS)
        xnT2 = sb("xnT2", DM, GC)
        lg = sb("lg", 128, GT, NE)
        lm = sb("lm", 128, GT)
        ls = sb("ls", 128, GT, NE)
        el = sb("el", 128, GT, NE)
        esum = sb("esum", 128, GT)
        einv = sb("einv", 128, GT)
        cmp = sb("cmp", 128, GT, NE, NE)
        tie = sb("tie", 128, GT, NE, NE)
        rank = sb("rank", 128, GT, NE)
        selw = sb("selw", 128, GT, NE)
        w9 = sb("w9", 128, GT, NX)
        w9T = sb("w9T", NX, GC)
        hh = [sb(f"hh{i}", 128, 2, GC) for i in range(2)]

        def bank(name):
            return ctx.enter_context(nc.psum_tensor(name, [128, 512], F32))
        BC = [bank("BC0"), bank("BC1")]
        GG = bank("GG")
        VT = bank("VT")
        RR = bank("RR")
        OO = bank("OO")
        YY = [RR, OO]
        HB = [bank("HB0"), bank("HB1")]
        NRM0 = 256

        ld_x = [sem(f"ld_x{g}") for g in range(NG)]
        ld_w, ld_f, st_out = sem("ld_w"), sem("ld_f"), sem("st_out")
        cst, cst_g, prep, prep_a = sem("cst"), sem("cst_g"), sem("prep"), sem("prep_a")
        taps_done = sem("taps_done")
        ln_var, ln_rstd, ln_xn = sem("ln_var"), sem("ln_rstd"), sem("ln_xn")
        h_ready, h_free = sem("h_ready"), sem("h_free")
        dt_e, dt_exp, dt_done = sem("dt_e"), sem("dt_exp"), sem("dt_done")
        sq_n, den_done, ln_den, lcum, de_done, ab_done = (sem(s) for s in
                                                         ("sq_n", "den_done", "ln_den", "lcum", "de_done", "ab_done"))
        uz_done, su_done = sem("uz_done"), sem("su_done")
        step = sem("step")
        bc_ready, yc_done, sq_done, vc_done, mul_done, wv_done = (sem(s) for s in
            ("bc_ready", "yc_done", "sq_done", "vc_done", "mul_done", "wv_done"))
        gv_done, gm_done, vt_done, nrm_done, ub_done = (sem(s) for s in
            ("gv_done", "gm_done", "vt_done", "nrm_done", "ub_done"))
        tail_done, z_done, y1_done, yg_done, ty_done, yt_done, op_done, x2_done, xi_done, tr_done = (sem(s) for s in
            ("tail_done", "z_done", "y1_done", "yg_done", "ty_done", "yt_done", "op_done", "x2_done", "xi_done",
             "tr_done"))
        lg_c, el_done, w9_done, y_ready, acc = (sem(s) for s in ("lg_c", "el_done", "w9_done", "y_ready", "acc"))
        dve_chain, pool_chain, halo = sem("dve_chain"), sem("pool_chain"), sem("halo")

        block = ctx.enter_context(nc.Block())
        LN1, LN2 = 0, 1

        def ln_index(kind, g):
            if kind == LN1:
                return max(2 * g - 1, 0)
            return 2 * g + 2 if g < NG - 1 else 2 * g + 1

        FRONT_USES, ROUTER_USES, EXPERT_USES = 2 + 1 + NH + GT, 3, 2 * NX
        F_USE, R_USE, T_USE = {0: 0}, {}, {ln_index(LN1, 0): 1}
        used = FRONT_USES
        for g in range(NG):
            if g + 1 < NG:
                F_USE[g + 1], T_USE[ln_index(LN1, g + 1)] = used, used + 1
                used += FRONT_USES
            R_USE[g], T_USE[ln_index(LN2, g)] = used, used + 1
            used += ROUTER_USES + EXPERT_USES

        @block.sync
        def _(sp):
            xv = x.rearrange("o (g c t) d -> (o g) t c d", g=NG, c=GT)
            ov = out.rearrange("o (g c t) d -> (o g) t c d", g=NG, c=GT)

            def dma_x(g):
                if g >= 3:
                    sp.wait_ge(st_out, 16 * (g - 2))
                sp.dma_start(xr[g % 3][:], xv[g]).then_inc(ld_x[g], 16)

            dma_x(0)
            sp.dma_start(winT[:, COL_U:COL_BC], w_inT[:, COL_U:COL_BC]).then_inc(ld_w, 16)
            sp.dma_start(taps[:], dw_wT.rearrange("(o k) d -> o k d", o=1).broadcast_to([128, TAPS, DI])).then_inc(ld_w, 16)
            sp.dma_start(dtbb[:], dt_bias.rearrange("(o h) -> o h", o=1).broadcast_to([128, NH])).then_inc(ld_w, 16)
            sp.dma_start(sgt[:, 0:NH], theta_rawT).then_inc(ld_w, 16)
            sp.dma_start(sgt[:, NH:2 * NH], k_rawT).then_inc(ld_w, 16)
            sp.dma_start(biasu[:], dw_b.rearrange("(o d) -> o d", o=1)).then_inc(ld_w, 16)
            sp.dma_start(skipb[:], skip.rearrange("(o d) -> o d", o=1).broadcast_to([128, DI])).then_inc(ld_w, 16)
            sp.dma_start(winT[:, 0:COL_U], w_inT[:, 0:COL_U]).then_inc(ld_w, 16)
            sp.dma_start(winT[:, COL_BC:], w_inT[:, COL_BC:]).then_inc(ld_w, 16)
            dma_x(1)
            dma_x(2)
            sp.dma_start(woT[:], w_outT.rearrange("(i d) m -> d i m", i=2)).then_inc(ld_f, 16)
            sp.dma_start(rw[:], router_w).then_inc(ld_f, 16)
            sp.dma_start(rb[:], router_b.rearrange("(o e) -> o e", o=1)).then_inc(ld_f, 16)
            sp.dma_start(w1[:, 0:NE, :], rw1.rearrange("e d h -> d e h")).then_inc(ld_f, 16)
            sp.dma_start(w1[:, NE, :], sw1).then_inc(ld_f, 16)
            sp.dma_start(b1[:, 0:NE, :], rb1T).then_inc(ld_f, 16)
            sp.dma_start(b1[:, NE, :], sb1T).then_inc(ld_f, 16)
            sp.dma_start(w2[:, 0:NE, :, :], rw2.rearrange("e (i h) d -> h e i d", i=2)).then_inc(ld_f, 16)
            sp.dma_start(w2[:, NE, :, :], sw2.rearrange("(i h) d -> h i d", i=2)).then_inc(ld_f, 16)
            sp.dma_start(b2[0:NE, :], rb2).then_inc(ld_f, 16)
            sp.dma_start(b2[NE:NX, :], sb2.rearrange("(o d) -> o d", o=1)).then_inc(ld_f, 16)
            for g in range(NG):
                sp.wait_ge(acc, GT * NX * (g + 1))
                sp.dma_start(ov[g], xr[g % 3][:]).then_inc(st_out, 16)
                if g + 3 < NG:
                    dma_x(g + 3)
            sp.wait_ge(st_out, 16 * NG)
        LD_W, LD_F = 9 * 16, 11 * 16

        @block.tensor
        def _(pe):
            uses = [0]

            def h_bank():
                n = uses[0]
                uses[0] += 1
                if n >= 2:
                    pe.wait_ge(h_free, n - 1)
                return HB[n % 2]

            def norm_T(kind, g):
                pe.wait_ge(ln_xn, ln_index(kind, g) + 1)
                hb = h_bank()
                for c in range(GT):
                    last = pe.transpose(hb[:, c * TS:(c + 1) * TS], xn[:, c, :], ident[:])
                last.then_inc(h_ready, 1)

            def front_dt(g):
                pe.wait_ge(h_free, uses[0])
                hb = h_bank()
                for c in range(GT):
                    last = pe.matmul(hb[:, NH * c:NH * c + NH], xnT[:, HALO + c * TS:HALO + (c + 1) * TS],
                                     winT[:, COL_DT:COL_DT + NH], start=True, stop=True)
                last.then_inc(h_ready, 1)

            def front_bcast(g):
                pe.wait_ge(dt_done, g + 1)
                hb = h_bank()
                pe.transpose(hb[0:KP, 0:TS], dtt[:], ident[:]).then_inc(h_ready, 1)
                pe.wait_ge(h_free, uses[0])
                for h in range(NH):
                    hb = h_bank()
                    for c in range(GT):
                        last = pe.matmul(hb[:, c * TS:(c + 1) * TS], ident[0:KP, NH * c + h:NH * c + h + 1].broadcast_to([KP, 128]), dtr[:],
                                         start=True, stop=True)
                    last.then_inc(h_ready, 1)

            def front_uz(g):
                if g == 0:
                    pe.wait_ge(taps_done, 1)
                xt = xnT
                for c in range(GT):
                    hb = h_bank()
                    for k in range(TAPS):
                        pe.matmul(hb[:, 0:DI], xt[:, c * TS + k:(c + 1) * TS + k], taps[:, k, :],
                                  start=(k == 0), stop=False)
                    pe.matmul(hb[:, 0:DI], onesrow[:], biasu[:], start=False, stop=True)
                    pe.matmul(hb[:, DI:2 * DI], xt[:, HALO + c * TS:HALO + (c + 1) * TS], winT[:, COL_Z:COL_Z + DI],
                              start=True, stop=True).then_inc(h_ready, 1)

            def router(g):
                pe.wait_ge(h_free, uses[0])
                hb = h_bank()
                for c in range(GT):
                    pe.matmul(hb[:, NE * c:NE * c + NE], xnT2[:, c * TS:(c + 1) * TS], rw[:],
                              start=True, stop=False)
                    last = pe.matmul(hb[:, NE * c:NE * c + NE], onesrow[:], rb[:], start=False, stop=True)
                last.then_inc(h_ready, 1)

            def router_T(g):
                pe.wait_ge(w9_done, g + 1)
                hb = h_bank()
                for c in range(GT):
                    last = pe.transpose(hb[0:NX, c * TS:(c + 1) * TS], w9[:, c, :], ident[:])
                last.then_inc(h_ready, 1)

            hid_free = {}

            def hidden(g, e):
                for i in range(2):
                    hb = h_bank()
                    pe.matmul(hb[:], w1[:, e, i * 128:(i + 1) * 128], xnT2[:], start=True, stop=True)\
                        .then_inc(h_ready, 1)
                hid_free[g, e] = uses[0]

            def expert_out(g, e):
                pe.wait_ge(h_free, hid_free[g, e])
                n = g * NX + e
                h = hh[n % 2]
                if n >= 2:
                    pe.wait_ge(acc, GT * (n - 1))
                yb = YY[n % 2]
                for c in range(GT):
                    for i in range(2):
                        last = pe.matmul(yb[:, c * TS:(c + 1) * TS], h[:, i, c * TS:(c + 1) * TS], w2[:, e, i, :],
                                         start=(i == 0), stop=(i == 1 and e != NE))
                    if e == NE:
                        last = pe.matmul(yb[:, c * TS:(c + 1) * TS], w9T[:, c * TS:(c + 1) * TS], b2[:],
                                         start=False, stop=True)
                last.then_inc(y_ready, 1)

            def proj(q):
                g, k = divmod(q, KP)
                c, h = divmod(k, NH)
                if q >= 2:
                    pe.wait_ge(sq_done, q - 1)
                b = BC[q % 2]
                xt = xnT[:, HALO + c * TS:HALO + (c + 1) * TS]
                for j in range(4):
                    col = COL_BC + h * 4 * NS + (0, 2, 1, 3)[j] * NS
                    last = pe.matmul(b[:, j * TS:(j + 1) * TS], winT[:, col:col + NS], xt, start=True, stop=True)
                last.then_inc(bc_ready, 1)

            def gv(q):
                h = q % NH
                tile = q // NH
                if q:
                    pe.wait_ge(gm_done, q)
                    pe.wait_ge(vt_done, q)
                if h == 0 and tile:
                    pe.wait_ge(nrm_done, tile)
                pe.wait_ge(sq_done, q + 1)
                for j in range(2):
                    for i in range(2):
                        pe.matmul(VT[:, NRM0 + NH * j + h:NRM0 + NH * j + h + 1], sq[q % 2][:, 2 * i + j, :], ones[:],
                                  start=(i == 0), stop=(i == 1))
                pe.wait_ge(wv_done, q + 1)
                v, w = vt[q % 2], wt[q % 8]
                for i in range(2):
                    pe.matmul(GG[:, 0:TS], v[:, i, :], w[:, i, :], start=(i == 0), stop=(i == 1))
                for i in range(2):
                    last = pe.transpose(VT[:, TS * i:TS * (1 + i)], v[:, i, :], ident[:])
                last.then_inc(gv_done, 1)

            def tail(tile):
                pe.wait_ge(ub_done, tile + 1)
                pe.wait_ge(vt_done, NH * (tile + 1))
                pe.wait_ge(gm_done, NH * (tile + 1))
                pe.wait_ge(xi_done, tile + 1)
                if tile:
                    pe.wait_ge(z_done, tile)
                    pe.wait_ge(x2_done, tile)
                    pe.wait_ge(acc, GT * NX * (tile // GT))
                u = ub[tile % 2]
                for h in range(NH):
                    q = NH * tile + h
                    hc = slice(h * HD, (h + 1) * HD)
                    for i in range(2):
                        pe.matmul(RR[:, i * DI + h * HD:i * DI + (h + 1) * HD], vts[q % 8][:, i, :], u[:, hc],
                                  start=True, stop=True)
                for h in range(NH):
                    q = NH * tile + h
                    hc = slice(h * HD, (h + 1) * HD)
                    pe.matmul(OO[:, hc], gts[q % 8][:], u[:, hc], start=True, stop=False)
                    for i in range(2):
                        last = pe.matmul(OO[:, hc], wt[q % 8][:, i, :], xi[tile % 2][:, i, hc],
                                         start=False, stop=(i == 1))
                last.then_inc(tail_done, 1)

            def ty(tile):
                pe.wait_ge(yg_done, tile + 1)
                if tile:
                    pe.wait_ge(yt_done, tile)
                for i in range(2):
                    last = pe.transpose(OO[:, DI + i * TS:DI + (i + 1) * TS], y3[:, i * 128:(i + 1) * 128], ident[:])
                last.then_inc(ty_done, 1)

            def op(tile):
                pe.wait_ge(yt_done, tile + 1)
                for i in range(2):
                    last = pe.matmul(OO[:, 0:DM], yT[:, i, :], woT[:, i, :], start=(i == 0), stop=(i == 1))
                last.then_inc(op_done, 1)

            def front(g):
                norm_T(LN1, g)
                front_dt(g)
                front_bcast(g)
                front_uz(g)

            pe.wait_ge(cst_g, 1)
            pe.wait_ge(ld_w, LD_W)
            front(0)
            pe.wait_ge(ld_f, LD_F)
            for g in range(NG):
                for k in range(KP):
                    q = KP * g + k
                    tile = q // NH
                    proj(q)
                    if k:
                        gv(q - 1)
                    if k > NH:
                        if k % NH == 0:
                            ty(tile - 2)
                        if k % NH == 1 and k > 2 * NH:
                            op(tile - 2)
                    if k > NH and k % NH == 2:
                        tail(tile - 1)
                last_tile = GT * (g + 1) - 1
                gv(KP * (g + 1) - 1)
                ty(last_tile - 1)
                op(last_tile - 1)
                tail(last_tile)
                ty(last_tile)
                op(last_tile)
                if g + 1 < NG:
                    front(g + 1)
                norm_T(LN2, g)
                router(g)
                router_T(g)
                for e in range(NX):
                    hidden(g, e)
                    if e:
                        expert_out(g, e - 1)
                expert_out(g, NE)

        @block.scalar
        def _(act):
            uses = [0]

            def h_read():
                n = uses[0]
                uses[0] += 1
                act.wait_ge(h_ready, n + 1)
                return HB[n % 2]

            def front(g):
                hb = h_read()
                xt = xnT
                if g:
                    act.wait_ge(h_free, uses[0] - 1)
                    act.activation(xt[:, 0:HALO], xt[:, GC:GC + HALO], ACT.Copy).then_inc(halo, 1)
                    act.wait_ge(halo, g)
                act.activation(xt[:, HALO:HALO + GC], hb[:], ACT.Copy).then_inc(h_free, 1)
                hb = h_read()
                act.activation(lraw[:], hb[:, 0:KP], ACT.Copy).then_inc(h_free, 1)
                act.wait_ge(dt_e, g + 1)
                act.activation(le[:], lx[:], ACT.Exp).then_inc(dt_exp, 1)
                hb = h_read()
                act.activation(dtr[:], hb[0:KP, 0:TS], ACT.Copy).then_inc(h_free, 1)
                if g:
                    act.wait_ge(step, STEP_OPS * g)
                for h in range(NH):
                    hb = h_read()
                    if g or h:
                        act.wait_ge(den_done, NH * g + h)
                    act.activation(sqn[:], hb[:].rearrange("p (c t) -> p c t", c=GT), ACT.Square,
                                   scale=theta[:, h:h + 1])
                    act.activation(view(ab, DTN + h * SL, (NH * SL, GT), (1, TS)),
                                   hb[:].rearrange("p (c t) -> p c t", c=GT), ACT.Copy).then_inc(h_free, 1)
                act.wait_ge(den_done, NH * (g + 1))
                act.activation(lden[:], lden[:], ACT.Ln, bias=1.0).then_inc(ln_den, 1)
                act.wait_ge(lcum, g + 1)
                act.activation(de[:, 0:PC], lden[:], ACT.Exp)
                act.activation(de[:, PC:2 * PC], lden[:], ACT.Exp, scale=-1.0).then_inc(de_done, 1)
                if g:
                    act.wait_ge(yg_done, GT * g)
                for c in range(GT):
                    hb = h_read()
                    act.activation(us[:, c, :], hb[:, 0:DI], ACT.Silu)
                    act.activation(sz[:, c, :], hb[:, DI:2 * DI], ACT.Silu).then_inc(h_free, 1)

            def pair(q):
                act.wait_ge(bc_ready, q + 1)
                if q >= 2:
                    act.wait_ge(mul_done, q - 1)
                b = BC[q % 2]
                act.activation(yc[q % 2][:], b[:].rearrange("p (j t) -> p j t", j=4), ACT.Copy)\
                    .then_inc(yc_done, 1)
                if q >= 2:
                    act.wait_ge(gv_done, q - 1)
                act.activation(sq[q % 2][:], b[:].rearrange("p (j t) -> p j t", j=4), ACT.Square).then_inc(sq_done, 1)

            def vt_copy(q):
                act.wait_ge(gv_done, q + 1)
                if q >= 8:
                    act.wait_ge(tail_done, (q - 8) // NH + 1)
                act.activation(vts[q % 8][:], VT[:, 0:2 * TS].rearrange("p (i n) -> p i n", i=2), ACT.Copy)\
                    .then_inc(vt_done, 1)
                if q % NH == NH - 1:
                    if q >= NH:
                        act.wait_ge(ub_done, q // NH)
                    act.activation(nrm[:], VT[:, NRM0:NRM0 + 8], ACT.Identity, bias=eps_l2[:]).then_inc(nrm_done, 1)

            def yT_copy(tile):
                act.wait_ge(ty_done, tile + 1)
                if tile:
                    act.wait_ge(op_done, tile)
                act.activation(yT[:], OO[:, DI:2 * DI].rearrange("p (i t) -> p i t", i=2), ACT.Copy)\
                    .then_inc(yt_done, 1)

            def norm2(g):
                hb = h_read()
                if g:
                    act.wait_ge(y_ready, NX * g)
                act.activation(xnT2[:], hb[:], ACT.Copy).then_inc(h_free, 1)

            def router(g):
                hb = h_read()
                act.activation(lg[:], hb[:, 0:GT * NE].rearrange("p (c e) -> p c e", c=GT), ACT.Copy)\
                    .then_inc(h_free, 1)
                act.wait_ge(lg_c, g + 1)
                act.activation(el[:], ls[:], ACT.Exp).then_inc(el_done, 1)
                hb = h_read()
                act.activation(w9T[:], hb[0:NX, :], ACT.Copy).then_inc(h_free, 1)

            def gelus(g, e):
                n = g * NX + e
                for i in range(2):
                    hb = h_read()
                    if i == 0 and n >= 2:
                        act.wait_ge(y_ready, n - 1)
                    act.activation(hh[n % 2][:, i, :], hb[:], ACT.Gelu, bias=b1[:, e, i:i + 1]).then_inc(h_free, 1)

            act.wait_ge(ld_w, LD_W)
            act.activation(sgt[:, 2 * NH:4 * NH], sgt[:, 0:2 * NH], ACT.Exp, scale=-1.0).then_inc(prep_a, 1)
            act.wait_ge(cst_g, 1)
            act.wait_ge(prep, 1)
            front(0)
            for g in range(NG):
                for k in range(KP):
                    q = KP * g + k
                    tile = q // NH
                    pair(q)
                    if k:
                        vt_copy(q - 1)
                    if k > NH and k % NH == 0:
                        yT_copy(tile - 2)
                last_tile = GT * (g + 1) - 1
                vt_copy(KP * (g + 1) - 1)
                yT_copy(last_tile - 1)
                yT_copy(last_tile)
                if g + 1 < NG:
                    front(g + 1)
                norm2(g)
                router(g)
                for e in range(NX):
                    gelus(g, e)

        @block.vector
        def _(dve):
            chain = [0]

            def link(ins):
                chain[0] += 1
                ins.then_inc(dve_chain, 1)
                dve.wait_ge(dve_chain, chain[0])

            def norm(kind, g):
                xg = xr[g % 3]
                if kind == LN1:
                    dve.wait_ge(ld_x[g], 16)
                for c in range(GT):
                    last = dve.bn_stats(stats[:, c, :], xg[:, c, :])
                link(last)
                for c in range(GT):
                    last = dve.bn_aggr(mv[:, c, :], stats[:, c, :])
                link(last)
                n = ln_index(kind, g)
                dve.tensor_scalar(mv[:, :, 1], mv[:, :, 1], EPS_LN, None, ALU.add).then_inc(ln_var, 1)
                dve.wait_ge(ln_rstd, n + 1)
                if n:
                    dve.wait_ge(h_ready, T_USE[n - 1])
                for c in range(GT):
                    last = dve.tensor_scalar(xn[:, c, :], xg[:, c, :], mv[:, c, 0:1], rstd[:, c:c + 1],
                                             ALU.subtract, ALU.mult)
                last.then_inc(ln_xn, 1)

            def front_dt(g):
                dve.wait_ge(h_free, F_USE[g] + 2)
                link(dve.tensor_tensor(lx[:].rearrange("p (c h) -> p c h", c=GT),
                                       lraw[:].rearrange("p (c h) -> p c h", c=GT),
                                       view(dtbb, 0, (0, GT), (1, NH)), ALU.add))
                dve.tensor_scalar(lx[:], lx[:], 0.0, None, ALU.min).then_inc(dt_e, 1)
                dve.wait_ge(dt_exp, g + 1)
                link(dve.tensor_scalar(le[:], le[:], E_MAX, None, ALU.min))
                link(dve.tensor_scalar(lp[0][:], le[:], 1.0 / 9, None, ALU.mult))
                for i, m in enumerate(range(8, 0, -1)):
                    c = (1.0 if m % 2 else -1.0) / m
                    link(dve.scalar_tensor_tensor(out=lp[(i + 1) % 2][:], in0=lp[i % 2][:], scalar=c, in1=le[:],
                                                  op0=ALU.add, op1=ALU.mult))
                if g:
                    dve.wait_ge(ub_done, GT * g)
                dve.tensor_scalar(dtt[:], lp[0][:], DT_MIN, DT_MAX, ALU.max, ALU.min).then_inc(dt_done, 1)

            def front_coef(g):
                dve.memset(view(lden, 0, (SL, KP), (1, 1)), 0.0)
                for h in range(NH):
                    dve.wait_ge(h_free, F_USE[g] + 4 + h)
                    dve.scalar_tensor_tensor(out=view(lden, h * SL + 1, (NH * SL, GT), (1, TS)),
                                             in0=view(ab, DTN + h * SL, (NH * SL, GT), (1, TS)), scalar=kvec[:, h:h + 1],
                                             in1=sqn[:], op0=ALU.mult, op1=ALU.add).then_inc(den_done, 1)
                dve.wait_ge(ln_den, g + 1)
                for k in range(KP):
                    last = dve.tensor_tensor_scan(ab[:, LCS + k * SL:LCS + (k + 1) * SL],
                                                  ones[:].broadcast_to([128, SL]), lden[:, k * SL:(k + 1) * SL],
                                                  0.0, ALU.mult, ALU.add)
                link(last)
                dve.tensor_tensor(view(lden, 0, (SL, KP), (1, SL)), view(ab, LCS, (SL, KP), (1, SL)),
                                  view(ab, LCS + MID, (SL, KP), (0, SL)), ALU.subtract).then_inc(lcum, 1)
                dve.wait_ge(de_done, g + 1)
                d = de
                link(dve.tensor_tensor(view(ab, PC + 1, (SL, KP), (1, TS)), view(d, PC + 1, (SL, KP), (1, TS)),
                                       view(ab, DTN, (SL, KP), (1, TS)), ALU.mult))
                for h in range(NH):
                    last = dve.scalar_tensor_tensor(out=view(ab, h * SL + 1, (NH * SL, GT), (1, TS)),
                                             in0=view(d, h * SL, (NH * SL, GT), (1, TS)), scalar=avec[:, h:h + 1],
                                             in1=view(ab, DTN + h * SL, (NH * SL, GT), (1, TS)),
                                                   op0=ALU.mult, op1=ALU.mult)
                last.then_inc(ab_done, 1)

            Y0, W0 = 0, 2 * PC
            issued = [0]

            def step_op(*args):
                dve.wait_ge(step, issued[0] - 1)
                dve.tensor_tensor(*args).then_inc(step, 1)
                issued[0] += 1

            def step_start(g):
                if g:
                    dve.wait_ge(wv_done, KP * g)
                dve.memset(view(pr, MID, (3 * PC, 2), (SL, KP)), 1.0)
                dve.memset(view(pr, PC + MID, (PC, 2), (SL, KP)), 0.0).then_inc(step, 1)
                issued[0] += 1
                dve.wait_ge(step, issued[0])
                dve.wait_ge(ab_done, g + 1)

            def one_step(j):
                lo, hi = MID - j, MID + j
                row = lambda o: view(pr, o, (PC, 2), (SL, KP))
                coef = lambda o: view(ab, o, (0, 2), (SL, KP))
                tmp = lambda t: t[:].rearrange("p (c k) -> p c k", c=2)
                step_op(tmp(ta[0]), coef(PC + lo), row(W0 + lo), ALU.mult)
                step_op(tmp(ta[1]), coef(hi + 1), row(Y0 + hi), ALU.mult)
                step_op(row(Y0 + lo - 1), row(Y0 + lo), tmp(ta[0]), ALU.subtract)
                step_op(row(W0 + hi + 1), row(W0 + hi), tmp(ta[1]), ALU.subtract)
                step_op(tmp(tb[0]), coef(lo), row(Y0 + lo - 1), ALU.mult)
                step_op(tmp(tb[1]), coef(PC + hi + 1), row(W0 + hi + 1), ALU.mult)
                step_op(row(W0 + lo - 1), row(W0 + lo), tmp(tb[0]), ALU.add)
                step_op(row(Y0 + hi + 1), row(Y0 + hi), tmp(tb[1]), ALU.add)

            def pair(q):
                g, k = divmod(q, KP)
                p, d = pr, de
                o = k * SL
                dve.wait_ge(yc_done, q + 1)
                dve.tensor_tensor(vc[q % 2][:], yc[q % 2][:, 2:4, :],
                                  view(d, o, (PC + 1, 2), (1, TS)), ALU.mult).then_inc(vc_done, 1)
                if q >= 2:
                    dve.wait_ge(wv_done, q - 1)
                m, y, v = mm[q % 2], yc[q % 2], vc[q % 2]
                over = lambda t, i: view(t, i * TS, (0, 2), (1, TS))
                dve.tensor_tensor(m[:, 0], over(y, 1), view(p, o + 1, (PC, 2), (1, TS)), ALU.mult)
                dve.tensor_tensor(m[:, 2], over(y, 0), view(p, W0 + o + 1, (PC, 2), (1, TS)), ALU.mult)
                dve.wait_ge(vc_done, q + 1)
                dve.tensor_tensor(m[:, 1], over(v, 1), view(p, W0 + o + 1, (PC, 2), (1, TS)), ALU.mult)
                dve.tensor_tensor(m[:, 3], over(v, 0), view(p, o, (PC, 2), (1, TS)), ALU.mult).then_inc(mul_done, 1)

            def gmask(q):
                dve.wait_ge(gv_done, q + 1)
                if q >= 8:
                    dve.wait_ge(tail_done, (q - 8) // NH + 1)
                dve.tensor_tensor(gts[q % 8][:], GG[:, 0:TS], causal[:], ALU.mult).then_inc(gm_done, 1)

            def tile_out(tile):
                dve.wait_ge(tail_done, tile + 1)
                if tile:
                    dve.wait_ge(xi_done, tile + 1)
                dve.tensor_tensor(zz[:], xi[tile % 2][:], RR[:].rearrange("p (i d) -> p i d", i=2), ALU.add)\
                    .then_inc(z_done, 1)
                if tile >= 2:
                    dve.wait_ge(yg_done, tile - 1)
                dve.tensor_tensor(y1[tile % 2][:].rearrange("p (h d) -> p h d", h=NH),
                                  OO[:, 0:DI].rearrange("p (h d) -> p h d", h=NH),
                                  view(rn[tile % 2], NH, (1, NH), (0, HD)), ALU.mult).then_inc(y1_done, 1)

            def residual(tile):
                dve.wait_ge(op_done, tile + 1)
                xg = xr[(tile // GT) % 3][:, tile % GT, :]
                dve.tensor_tensor(xg, OO[:, 0:DM], xg, ALU.add).then_inc(x2_done, 1)

            def router(g):
                dve.wait_ge(h_free, R_USE[g] + 2)
                link(dve.tensor_reduce(lm[:], lg[:], AX.X, ALU.max))
                dve.tensor_tensor(ls[:], lg[:], view(lm, 0, (1, GT), (0, NE)), ALU.subtract).then_inc(lg_c, 1)
                lj = view(lg, 0, (NE, GT), (0, NE), (1, NE))
                li = view(lg, 0, (NE, GT), (1, NE), (0, NE))
                dve.tensor_tensor(cmp[:], lj, li, ALU.is_gt)
                link(dve.tensor_tensor(tie[:], lj, li, ALU.is_equal))
                flat = lambda t: t[:].rearrange("p c e j -> p c (e j)")
                link(dve.tensor_tensor(flat(tie), flat(tie), view(before, 0, (0, GT), (1, NE * NE)), ALU.mult))
                link(dve.tensor_tensor(cmp[:], cmp[:], tie[:], ALU.add))
                link(dve.tensor_reduce(rank[:], cmp[:], AX.X, ALU.add))
                dve.wait_ge(el_done, g + 1)
                link(dve.tensor_reduce(esum[:], el[:], AX.X, ALU.add))
                link(dve.reciprocal(einv[:], esum[:]))
                link(dve.scalar_tensor_tensor(out=selw[:], in0=rank[:], scalar=1.5, in1=el[:],
                                              op0=ALU.is_lt, op1=ALU.mult))
                if g:
                    dve.wait_ge(acc, GT * NX * g)
                dve.memset(w9[:, :, NE:NX], 1.0)
                dve.tensor_tensor(w9[:, :, 0:NE], selw[:], view(einv, 0, (1, GT), (0, NE)), ALU.mult)\
                    .then_inc(w9_done, 1)

            def add_expert(g, e):
                n = g * NX + e
                dve.wait_ge(y_ready, n + 1)
                yb = YY[n % 2]
                for c in range(GT):
                    if e:
                        dve.wait_ge(acc, GT * (n - 1) + c + 1)
                    xg = xr[g % 3][:, c, :]
                    dve.scalar_tensor_tensor(out=xg, in0=yb[:, c * TS:(c + 1) * TS], scalar=w9[:, c, e:e + 1],
                                             in1=xg, op0=ALU.mult, op1=ALU.add).then_inc(acc, 1)

            dve.wait_ge(ld_w, LD_W)
            dve.memset(ones[:], 1.0)
            dve.memset(onesrow[:], 1.0)
            dve.memset(mhalf[:], -0.5)
            dve.memset(eps_l2[:], EPS_L2)
            dve.memset(xnT[:, 0:HALO], 0.0)
            dve.memset(lden[:], 0.0).then_inc(cst, 1)
            dve.wait_ge(cst, 1)
            dve.wait_ge(prep_a, 1)
            link(dve.tensor_scalar(sgt[:, 2 * NH:], sgt[:, 2 * NH:], 1.0, None, ALU.add))
            link(dve.reciprocal(sgt[:, 2 * NH:], sgt[:, 2 * NH:]))
            dve.tensor_scalar(kvec[:], sgt[:, 3 * NH:], K_MAX, None, ALU.mult)
            link(dve.tensor_scalar(theta[:], sgt[:, 2 * NH:3 * NH], PI, None, ALU.mult))
            dve.tensor_tensor(avec[:], theta[:], theta[:], ALU.mult).then_inc(prep, 1)
            dve.wait_ge(prep, 1)
            norm(LN1, 0)
            for k in range(TAPS):
                last = dve.tensor_tensor(taps[:, k, :], taps[:, k, :], winT[:, COL_U:COL_U + DI], ALU.mult)
            last.then_inc(taps_done, 1)
            front_dt(0)
            front_coef(0)
            for g in range(NG):
                step_start(g)
                for j in range(MID):
                    one_step(j)
                    if g and j % STEPS_PER_EXPERT == STEPS_PER_EXPERT - 1:
                        add_expert(g - 1, j // STEPS_PER_EXPERT)
                dve.wait_ge(step, STEP_OPS * (g + 1))
                for k in range(KP):
                    q = KP * g + k
                    tile = q // NH
                    pair(q)
                    if k:
                        gmask(q - 1)
                    if k > NH:
                        if k % NH == 3:
                            tile_out(tile - 1)
                        if k % NH == 2 and k > 2 * NH:
                            residual(tile - 2)
                last_tile = GT * (g + 1) - 1
                gmask(KP * (g + 1) - 1)
                residual(last_tile - 1)
                tile_out(last_tile)
                residual(last_tile)
                dve.wait_ge(x2_done, last_tile + 1)
                if g + 1 < NG:
                    norm(LN1, g + 1)
                    front_dt(g + 1)
                    front_coef(g + 1)
                norm(LN2, g)
                router(g)
            for e in range(NX):
                add_expert(NG - 1, e)

        @block.gpsimd
        def _(pool):
            chain = [0]

            def link(ins):
                chain[0] += 1
                ins.then_inc(pool_chain, 1)
                pool.wait_ge(pool_chain, chain[0])

            def rstd_of(n):
                pool.wait_ge(ln_var, n + 1)
                if n:
                    pool.wait_ge(ln_xn, n)
                pool.tensor_tensor(rstd[:], mv[:, :, 1], mhalf[:, 0:GT], ALU.pow).then_inc(ln_rstd, 1)

            def crossings(g):
                pool.wait_ge(step, STEP_OPS * (g + 1))
                p, d = pr, de
                W0 = 2 * PC
                if g:
                    link(pool.tensor_copy(edge[:, :, 0:NH], edge[:, :, KP:KP + NH]))
                pool.tensor_copy(edge[:, 0:2, NH:], view(p, TS, (PC, 2), (SL, KP)))
                link(pool.tensor_tensor(edge[:, 2:4, NH:], view(p, W0 + TS, (PC, 2), (SL, KP)),
                                        view(d, PC + TS, (0, 2), (SL, KP)), ALU.mult))
                link(pool.tensor_tensor(ew[:], edge[:, 2:4, 0:KP], view(d, 0, (0, 2), (SL, KP)), ALU.mult))
                first = lambda o: view(p, o, (0, 2), (SL, KP))
                y = edge[:, 0:2, 0:KP]
                pool.tensor_tensor(tra[:, 0], first(W0 + PC), y, ALU.mult)
                pool.tensor_tensor(tra[:, 1], first(PC), ew[:], ALU.mult)
                pool.tensor_tensor(tra[:, 2], first(0), ew[:], ALU.mult)
                link(pool.tensor_tensor(tra[:, 3], first(W0), y, ALU.mult))
                pool.tensor_tensor(tr[:, :, 0, :], tra[:, 0], tra[:, 1], ALU.subtract)
                link(pool.tensor_tensor(tr[:, :, 1, :], tra[:, 2], tra[:, 3], ALU.subtract))

            def wv(q):
                pool.wait_ge(mul_done, q + 1)
                if q >= 8:
                    pool.wait_ge(tail_done, (q - 8) // NH + 1)
                m = mm[q % 2]
                pool.tensor_tensor(wt[q % 8][:], m[:, 0], m[:, 1], ALU.add)
                if q >= 2:
                    pool.wait_ge(gv_done, q - 1)
                pool.tensor_tensor(vt[q % 2][:, 0, :], m[:, 2, 1, :], m[:, 3, 1, :], ALU.subtract)
                pool.tensor_tensor(vt[q % 2][:, 1, :], m[:, 3, 0, :], m[:, 2, 0, :], ALU.subtract).then_inc(wv_done, 1)

            def ubar(tile):
                pool.wait_ge(nrm_done, tile + 1)
                g, c = divmod(tile, GT)
                if tile >= 2:
                    pool.wait_ge(y1_done, tile - 1)
                    pool.wait_ge(tail_done, tile - 1)
                link(pool.tensor_tensor(rn[tile % 2][:], nrm[:], mhalf[:], ALU.pow))
                link(pool.tensor_tensor(du[:], rn[tile % 2][:, 0:NH], dtt[:, NH * c:NH * c + NH], ALU.mult))
                pool.tensor_tensor(ub[tile % 2][:].rearrange("p (h d) -> p h d", h=NH),
                                   us[:, c, :].rearrange("p (h d) -> p h d", h=NH),
                                   view(du, 0, (1, NH), (0, HD)), ALU.mult).then_inc(ub_done, 1)
                pool.tensor_tensor(su[tile % 2][:], us[:, c, :], skipb[:], ALU.mult).then_inc(su_done, 1)

            def gate(tile):
                g, c = divmod(tile, GT)
                pool.wait_ge(y1_done, tile + 1)
                pool.wait_ge(su_done, tile + 1)
                link(pool.tensor_tensor(y2[:], y1[tile % 2][:], su[tile % 2][:], ALU.add))
                if tile:
                    pool.wait_ge(ty_done, tile)
                pool.tensor_tensor(y3[:], y2[:], sz[:, c, :], ALU.mult).then_inc(yg_done, 1)

            def state(tile):
                k = NH * (tile % GT)
                pool.wait_ge(z_done, tile)
                pick = lambda col: view(tr, col * 2 * KP + k, (KP, 2), (1, NH), (0, HD))
                full = lambda t: t[:].rearrange("p i (h d) -> p i h d", h=NH)
                pool.tensor_tensor(full(x1), pick(0), view(zz, 0, (0, 2), (HD, NH), (1, HD)), ALU.mult)
                link(pool.tensor_tensor(full(x2), pick(1), view(zz, DI, (0, 2), (HD, NH), (1, HD)), ALU.mult))
                pool.tensor_tensor(xi[tile % 2][:], x1[:], x2[:], ALU.add).then_inc(xi_done, 1)

            pool.memset(xi[0][:], 0.0).then_inc(xi_done, 1)
            pool.memset(edge[:], 0.0)
            pool.memset(ident[:], 0.0)
            pool.memset(causal[:], 1.0)
            link(pool.memset(before[:], 1.0))
            pool.affine_select(out=ident[:], in_=ident[:], compare_op=ALU.not_equal, fill=1.0, base=0,
                               pattern=[[-1, 128]], channel_multiplier=1)
            pool.affine_select(out=causal[:], in_=causal[:], compare_op=ALU.is_ge, fill=0.0, base=0,
                               pattern=[[1, 128]], channel_multiplier=-1)
            link(pool.affine_select(out=before[:], in_=before[:], compare_op=ALU.is_gt, fill=0.0, base=0,
                                    pattern=[[1, NE], [-1, NE]], channel_multiplier=0))
            pool.wait_ge(cst, 1)
            pool.memset(ew[:], 0.0).then_inc(cst_g, 1)
            rstd_of(0)
            for g in range(NG):
                crossings(g)
                for k in range(KP):
                    q = KP * g + k
                    tile = q // NH
                    wv(q)
                    if k >= NH and k % NH == 1:
                        ubar(tile - 1)
                    if k % NH == 3:
                        if tile:
                            state(tile)
                        if k >= NH:
                            gate(tile - 1)
                last_tile = GT * (g + 1) - 1
                ubar(last_tile)
                gate(last_tile)
                if g + 1 < NG:
                    rstd_of(ln_index(LN1, g + 1))
                rstd_of(ln_index(LN2, g))


def kernel(**inputs):
    import numpy as np
    import concourse.bacc as bacc
    from concourse.bass_utils import run_bass_kernel_spmd

    a = {n.split("_", 1)[1]: np.asarray(v) for n, v in inputs.items()}
    hidden_cols = lambda v: v.reshape(-1, 2, 128).transpose(2, 0, 1)
    laid = {
        "x": a["attn_x"], "w_inT": a["attn_W_in"].T, "dw_wT": a["attn_dw_weight"].T, "dw_b": a["attn_dw_bias"],
        "w_outT": a["attn_W_out"].T, "skip": a["attn_skip"], "dt_bias": a["attn_dt_bias"],
        "theta_rawT": a["attn_theta_raw"].T, "k_rawT": a["attn_k_raw"].T,
        "router_w": a["ffn_router_w"], "router_b": a["ffn_router_b"],
        "sw1": a["ffn_sw1"], "sb1T": hidden_cols(a["ffn_sb1"])[:, 0], "sw2": a["ffn_sw2"], "sb2": a["ffn_sb2"],
        "rw1": a["ffn_rw1"], "rb1T": hidden_cols(a["ffn_rb1"]), "rw2": a["ffn_rw2"], "rb2": a["ffn_rb2"],
    }
    nc = bacc.Bacc("TRN2", target_bir_lowering=False, num_devices=1)
    arrays, args = {}, {}
    for name, v in laid.items():
        v = np.ascontiguousarray(v)
        arrays[f"in_{name}"] = v
        args[name] = nc.dram_tensor(f"in_{name}", v.shape, mybir.dt.from_np(v.dtype), kind="ExternalInput").ap()
    args["out"] = nc.dram_tensor("out_0", (1, T, DM), F32, kind="ExternalOutput").ap()
    build(nc, **args)
    r = run_bass_kernel_spmd(nc, [arrays], core_ids=[0])
    return r.results[0]["out_0"]
```

```python
from contextlib import ExitStack

import concourse.bass as bass
from concourse import mybir

F32 = mybir.dt.float32
ALU = mybir.AluOpType
ACT = mybir.ActivationFunctionType
AX = mybir.AxisListType

T, DM = 2048, 128
NH, HD, NS = 4, 64, 128
DI = NH * HD
TAPS = 4
NE, NX, HF = 8, 9, 256
TS = 128
GT = 4
NT, NG = T // TS, T // (TS * GT)
KP = GT * NH
GC = GT * TS
SL = TS + 1
MID = TS // 2
PC = KP * SL
DT_MIN, DT_MAX = 1e-4, 0.1
E_MAX = 0.11
PI = 3.141592653589793
K_MAX = 0.5
EPS_LN, EPS_L2 = 1e-5, 1e-8
HALO = TAPS - 1
COL_Z, COL_U, COL_DT, COL_BC = 0, DI, 2 * DI, 2 * DI + NH
DS = MID // 2
EXPERT_EVERY = 3
STEP_OPS = 6 * DS + 1


def view(t, offset, *dims):
    full = t[:]
    return bass.AP(tensor=full.tensor, offset=full.offset + offset,
                   ap=[list(full.ap[0])] + [[s, n] for s, n in dims])


def build(nc, x, w_inT, dw_wT, dw_b, w_outT, skipT_in, dt_bias, theta_rawT, k_rawT,
          router_w, router_b, sw1, sb1T, sw2, sb2, rw1, rb1T, rw2, rb2, out):
    ctx = ExitStack()
    with ctx:
        def sb(name, *shape, dtype=F32):
            return ctx.enter_context(nc.sbuf_tensor(name, list(shape), dtype))

        def sem(name):
            return ctx.enter_context(nc.semaphore(name))

        winT = sb("winT", DM, 2 * DI + NH + 4 * NH * NS)
        taps = sb("taps", DM, TAPS, DI)
        biasu = sb("biasu", 1, DI)
        woT = sb("woT", 128, 2, DM)
        skipT = sb("skipT", 128, 2)
        dtbb = sb("dtbb", 128, NH)
        theta = sb("theta", NS, NH)
        avec = sb("avec", NS, NH)
        kvec = sb("kvec", NS, NH)
        sgt = sb("sgt", NS, 4 * NH)
        rw = sb("rw", DM, NE)
        rb = sb("rb", 1, NE)
        w1 = sb("w1", DM, NX, HF)
        b1 = sb("b1", 128, NX, 2)
        w2 = sb("w2", 128, NX, 2, DM)
        b2 = sb("b2", NX, DM)
        ident = sb("ident", 128, 128)
        causal = sb("causal", 128, 128)
        before = sb("before", 128, NE, NE)
        ones = sb("ones", 128, 1)
        rowsel = sb("rowsel", 128, 2, 128)
        onesrow = sb("onesrow", 1, 128)
        eps_l2 = sb("eps_l2", 128, 1)
        mhalf = sb("mhalf", 128, 8)
        xr = [sb(f"xr{i}", 128, GT, DM) for i in range(3)]
        xn = sb("xn", 128, GT, DM)
        xnT = sb("xnT", DM, HALO + GC)
        stats = sb("stats", 128, GT, 6)
        mv = sb("mv", 128, GT, 2)
        rstd = sb("rstd", 128, GT)
        lraw = sb("lraw", 128, KP)
        lx = sb("lx", 128, KP)
        le = sb("le", 128, KP)
        lp = [sb(f"lp{i}", 128, KP) for i in range(2)]
        dtt = sb("dtt", 128, KP)
        dtr = sb("dtr", KP, TS)
        sqn = sb("sqn", NS, GT, TS)
        lden = sb("lden", NS, PC)
        de = sb("de", NS, 2 * PC)
        ab = sb("ab", NS, 2 * PC)
        DTN, LCS = 1, PC
        szT = sb("szT", 128, 2, GC)
        uT = sb("uT", 128, 2, GC)
        us = sb("us", 128, GT, DI)
        pr = sb("pr", NS, 4 * PC)
        ta = [sb(f"ta{i}", NS, 4 * KP) for i in range(2)]
        tb = [sb(f"tb{i}", NS, 4 * KP) for i in range(2)]
        tf = [sb(f"tf{i}", NS, 2 * NH * DS) for i in range(2)]
        yc = [sb(f"yc{i}", NS, 4, TS) for i in range(2)]
        sqs = sb("sqs", NS, 2 * 4 * TS)
        sq = [sqs[:, i * 4 * TS:(i + 1) * 4 * TS].rearrange("p (j t) -> p j t", j=4)
              for i in range(2)]
        vc = [sb(f"vc{i}", NS, 2, TS) for i in range(2)]
        mm = [sb(f"mm{i}", NS, 4, 2, TS) for i in range(2)]
        big = sb("big", 128, 16 * 2 * TS)
        part = lambda i: big[:, i * 2 * TS:(i + 1) * 2 * TS].rearrange("p (i t) -> p i t", i=2)
        wt = [part(i) for i in range(8)]
        vt = [sb(f"vt{i}", NS, 2, TS) for i in range(2)]
        vts = [part(8 + i) for i in range(8)]
        gtm = sb("gtm", TS, 8 * TS)
        gts = [gtm[:, i * TS:(i + 1) * TS] for i in range(8)]
        rlog = sb("rlog", 128, 2, TS)
        rrow = sb("rrow", 128, 2, TS)
        rbt = sb("rbt", 128, NH)
        rcb = sb("rcb", 128, 2, TS)
        gate = [sb(f"gate{i}", 128, 2, TS) for i in range(2)]
        rts = sb("rts", 128, 2, 2, NS)
        du = sb("du", 128, NH)
        ub = [sb(f"ub{i}", 128, DI) for i in range(2)]
        xi = [sb(f"xi{i}", NS, 2, DI) for i in range(2)]
        zz = sb("zz", NS, 2, DI)
        x1 = sb("x1", NS, 2, DI)
        x2 = sb("x2", NS, 2, DI)
        edge = sb("edge", NS, 4, NH + KP)
        ew = sb("ew", NS, 2, KP)
        tra = sb("tra", NS, 4, 2, KP)
        tr = sb("tr", NS, 2, 2, KP)
        y1 = [sb(f"y1{i}", 128, 2, TS) for i in range(2)]
        y3 = [sb(f"y3{i}", 128, 2, TS) for i in range(2)]
        xnT2 = sb("xnT2", DM, GC)
        lg = sb("lg", 128, GT, NE)
        lm = sb("lm", 128, GT)
        ls = sb("ls", 128, GT, NE)
        el = sb("el", 128, GT, NE)
        esum = sb("esum", 128, GT)
        einv = sb("einv", 128, GT)
        cmp, tie = (t[:].rearrange("p (c e j) -> p c e j", c=GT, e=NE) for t in tf)
        rank = sb("rank", 128, GT, NE)
        selw = sb("selw", 128, GT, NE)
        w9 = sb("w9", 128, GT, NX)
        w9T = sb("w9T", NX, GC)
        hh = [t[:].rearrange("p (i t) -> p i t", i=2) for t in (gtm, sqs)]

        def bank(name):
            return ctx.enter_context(nc.psum_tensor(name, [128, 512], F32))
        BC = [bank("BC0"), bank("BC1")]
        GG = bank("GG")
        VT = bank("VT")
        RR = bank("RR")
        OO = bank("OO")
        YY = [RR, OO]
        HB = [bank("HB0"), bank("HB1")]
        NRM0 = 256

        ld_x = [sem(f"ld_x{g}") for g in range(NG)]
        ld_w, ld_f, st_out = sem("ld_w"), sem("ld_f"), sem("st_out")
        cst, cst_g, prep, prep_a = sem("cst"), sem("cst_g"), sem("prep"), sem("prep_a")
        taps_done = sem("taps_done")
        ln_var, ln_rstd, ln_xn = sem("ln_var"), sem("ln_rstd"), sem("ln_xn")
        h_ready, h_free = sem("h_ready"), sem("h_free")
        dt_e, dt_exp, dt_done = sem("dt_e"), sem("dt_exp"), sem("dt_done")
        sq_n, den_done, ln_den, lcum, de_done, ab_done = (sem(s) for s in
                                                         ("sq_n", "den_done", "ln_den", "lcum", "de_done", "ab_done"))
        skip_done = sem("skip_done")
        row_log = sem("row_log")
        mat_p, mat_d, mat_e, step, fill = sem("mat_p"), sem("mat_d"), sem("mat_e"), sem("step"), sem("fill")
        bc_ready, yc_done, sq_done, vc_done, mul_done, wv_done = (sem(s) for s in
            ("bc_ready", "yc_done", "sq_done", "vc_done", "mul_done", "wv_done"))
        gv_done, gm_done, vt_done, row_done, nb_done, ub_done, gate_done = (sem(s) for s in
            ("gv_done", "gm_done", "vt_done", "row_done", "nb_done", "ub_done", "gate_done"))
        r_done, tail_done, rts_done, rt_done, z_done, y1_done, y3_done, op_done, x2_done, xi_done = (sem(s) for s in
            ("r_done", "tail_done", "rts_done", "rt_done", "z_done", "y1_done", "y3_done", "op_done", "x2_done",
             "xi_done"))
        lg_c, el_done, w9_done, y_ready, acc = (sem(s) for s in ("lg_c", "el_done", "w9_done", "y_ready", "acc"))
        dve_chain, pool_chain, halo = sem("dve_chain"), sem("pool_chain"), sem("halo")

        def coef2(f, kind, second):
            slot = MID + 1 + second if f else MID - second
            return view(ab, kind * PC + slot, (2 if f else -2, DS), (SL, KP))

        c1 = lambda f, second: coef2(f, 1 - f, second)
        c2 = lambda f, second: coef2(f, f, second)

        def entry(f, row, operand):
            comp = lambda role: f if role == "x" else 1 - f
            return view(big, ((2 * f + comp(operand)) * 2 + comp(row)) * DS * KP, (KP, DS), (1, KP))

        scr = lambda f, i: view(mm[f], i * DS * KP, (KP, DS), (1, KP))
        scr_p = lambda f: view(yc[f], 0, (KP, DS), (1, KP))

        block = ctx.enter_context(nc.Block())
        LN1, LN2 = 0, 1

        def ln_index(kind, g):
            if kind == LN1:
                return max(2 * g - 1, 0)
            return 2 * g + 2 if g < NG - 1 else 2 * g + 1

        FRONT_USES, MID_USES, ROUTER_USES, EXPERT_USES = 3 + NH + 6, GT, 3, 2 * NX
        F_USE, M_USE, R_USE, T_USE = {0: 0}, {}, {}, {ln_index(LN1, 0): 1}
        used = FRONT_USES
        for g in range(NG):
            M_USE[g] = used
            used += MID_USES
            if g + 1 < NG:
                F_USE[g + 1], T_USE[ln_index(LN1, g + 1)] = used, used + 1
                used += FRONT_USES
            R_USE[g], T_USE[ln_index(LN2, g)] = used, used + 1
            used += ROUTER_USES + EXPERT_USES

        @block.sync
        def _(sp):
            xv = x.rearrange("o (g c t) d -> (o g) t c d", g=NG, c=GT)
            ov = out.rearrange("o (g c t) d -> (o g) t c d", g=NG, c=GT)

            def dma_x(g):
                if g >= 3:
                    sp.wait_ge(st_out, 16 * (g - 2))
                sp.dma_start(xr[g % 3][:], xv[g]).then_inc(ld_x[g], 16)

            dma_x(0)
            sp.dma_start(winT[:, COL_U:COL_BC], w_inT[:, COL_U:COL_BC]).then_inc(ld_w, 16)
            sp.dma_start(taps[:], dw_wT.rearrange("(o k) d -> o k d", o=1).broadcast_to([128, TAPS, DI])).then_inc(ld_w, 16)
            sp.dma_start(dtbb[:], dt_bias.rearrange("(o h) -> o h", o=1).broadcast_to([128, NH])).then_inc(ld_w, 16)
            sp.dma_start(sgt[:, 0:NH], theta_rawT).then_inc(ld_w, 16)
            sp.dma_start(sgt[:, NH:2 * NH], k_rawT).then_inc(ld_w, 16)
            sp.dma_start(biasu[:], dw_b.rearrange("(o d) -> o d", o=1)).then_inc(ld_w, 16)
            sp.dma_start(skipT[:], skipT_in).then_inc(ld_w, 16)
            sp.dma_start(winT[:, 0:COL_U], w_inT[:, 0:COL_U]).then_inc(ld_w, 16)
            sp.dma_start(winT[:, COL_BC:], w_inT[:, COL_BC:]).then_inc(ld_w, 16)
            dma_x(1)
            dma_x(2)
            sp.dma_start(woT[:], w_outT.rearrange("(i d) m -> d i m", i=2)).then_inc(ld_f, 16)
            sp.dma_start(rw[:], router_w).then_inc(ld_f, 16)
            sp.dma_start(rb[:], router_b.rearrange("(o e) -> o e", o=1)).then_inc(ld_f, 16)
            sp.dma_start(w1[:, 0:NE, :], rw1.rearrange("e d h -> d e h")).then_inc(ld_f, 16)
            sp.dma_start(w1[:, NE, :], sw1).then_inc(ld_f, 16)
            sp.dma_start(b1[:, 0:NE, :], rb1T).then_inc(ld_f, 16)
            sp.dma_start(b1[:, NE, :], sb1T).then_inc(ld_f, 16)
            sp.dma_start(w2[:, 0:NE, :, :], rw2.rearrange("e (i h) d -> h e i d", i=2)).then_inc(ld_f, 16)
            sp.dma_start(w2[:, NE, :, :], sw2.rearrange("(i h) d -> h i d", i=2)).then_inc(ld_f, 16)
            sp.dma_start(b2[0:NE, :], rb2).then_inc(ld_f, 16)
            sp.dma_start(b2[NE:NX, :], sb2.rearrange("(o d) -> o d", o=1)).then_inc(ld_f, 16)
            for g in range(NG):
                sp.wait_ge(acc, GT * NX * (g + 1))
                sp.dma_start(ov[g], xr[g % 3][:]).then_inc(st_out, 16)
                if g + 3 < NG:
                    dma_x(g + 3)
            sp.wait_ge(st_out, 16 * NG)
        LD_W, LD_F = 9 * 16, 11 * 16

        @block.tensor
        def _(pe):
            uses = [0]

            def h_bank():
                n = uses[0]
                uses[0] += 1
                if n >= 2:
                    pe.wait_ge(h_free, n - 1)
                return HB[n % 2]

            def norm_T(kind, g):
                pe.wait_ge(ln_xn, ln_index(kind, g) + 1)
                hb = h_bank()
                for c in range(GT):
                    last = pe.transpose(hb[:, c * TS:(c + 1) * TS], xn[:, c, :], ident[:])
                last.then_inc(h_ready, 1)

            def front_dt(g):
                pe.wait_ge(h_free, uses[0])
                hb = h_bank()
                for c in range(GT):
                    last = pe.matmul(hb[:, NH * c:NH * c + NH], xnT[:, HALO + c * TS:HALO + (c + 1) * TS],
                                     winT[:, COL_DT:COL_DT + NH], start=True, stop=True)
                last.then_inc(h_ready, 1)

            def front_bcast(g):
                pe.wait_ge(dt_done, g + 1)
                hb = h_bank()
                pe.transpose(hb[0:KP, 0:TS], dtt[:], ident[:]).then_inc(h_ready, 1)
                pe.wait_ge(h_free, uses[0])
                for h in range(NH):
                    hb = h_bank()
                    for c in range(GT):
                        last = pe.matmul(hb[:, c * TS:(c + 1) * TS], ident[0:KP, NH * c + h:NH * c + h + 1].broadcast_to([KP, 128]), dtr[:],
                                         start=True, stop=True)
                    last.then_inc(h_ready, 1)

            def front_uz(g):
                if g == 0:
                    pe.wait_ge(taps_done, 1)
                for c2 in range(GT // 2):
                    hb = h_bank()
                    for c in (2 * c2, 2 * c2 + 1):
                        o = hb[:, (c % 2) * DI:(c % 2 + 1) * DI]
                        for k in range(TAPS):
                            pe.matmul(o, xnT[:, c * TS + k:(c + 1) * TS + k], taps[:, k, :],
                                      start=(k == 0), stop=False)
                        last = pe.matmul(o, onesrow[:], biasu[:], start=False, stop=True)
                    last.then_inc(h_ready, 1)
                for i in range(2):
                    hb = h_bank()
                    pe.matmul(hb[:], winT[:, COL_Z + i * 128:COL_Z + (i + 1) * 128], xnT[:, HALO:HALO + GC],
                              start=True, stop=True).then_inc(h_ready, 1)
                pe.wait_ge(h_free, F_USE[g] + 3 + NH + 2)
                for i in range(2):
                    hb = h_bank()
                    for c in range(GT):
                        last = pe.transpose(hb[:, c * TS:(c + 1) * TS], us[:, c, i * 128:(i + 1) * 128], ident[:])
                    last.then_inc(h_ready, 1)

            def router(g):
                pe.wait_ge(h_free, uses[0])
                hb = h_bank()
                for c in range(GT):
                    pe.matmul(hb[:, NE * c:NE * c + NE], xnT2[:, c * TS:(c + 1) * TS], rw[:],
                              start=True, stop=False)
                    last = pe.matmul(hb[:, NE * c:NE * c + NE], onesrow[:], rb[:], start=False, stop=True)
                last.then_inc(h_ready, 1)

            def router_T(g):
                pe.wait_ge(w9_done, g + 1)
                hb = h_bank()
                for c in range(GT):
                    last = pe.transpose(hb[0:NX, c * TS:(c + 1) * TS], w9[:, c, :], ident[:])
                last.then_inc(h_ready, 1)

            hid_free = {}

            def hidden(g, e):
                for i in range(2):
                    hb = h_bank()
                    pe.matmul(hb[:], w1[:, e, i * 128:(i + 1) * 128], xnT2[:], start=True, stop=True)\
                        .then_inc(h_ready, 1)
                hid_free[g, e] = uses[0]

            def expert_out(g, e):
                pe.wait_ge(h_free, hid_free[g, e])
                n = g * NX + e
                h = hh[n % 2]
                if n >= 2:
                    pe.wait_ge(acc, GT * (n - 1))
                yb = YY[n % 2]
                for c in range(GT):
                    for i in range(2):
                        last = pe.matmul(yb[:, c * TS:(c + 1) * TS], h[:, i, c * TS:(c + 1) * TS], w2[:, e, i, :],
                                         start=(i == 0), stop=(i == 1 and e != NE))
                    if e == NE:
                        last = pe.matmul(yb[:, c * TS:(c + 1) * TS], w9T[:, c * TS:(c + 1) * TS], b2[:],
                                         start=False, stop=True)
                last.then_inc(y_ready, 1)

            def proj(q):
                g, k = divmod(q, KP)
                c, h = divmod(k, NH)
                if q >= 2:
                    pe.wait_ge(sq_done, q - 1)
                b = BC[q % 2]
                xt = xnT[:, HALO + c * TS:HALO + (c + 1) * TS]
                for j in range(4):
                    col = COL_BC + h * 4 * NS + (0, 2, 1, 3)[j] * NS
                    last = pe.matmul(b[:, j * TS:(j + 1) * TS], winT[:, col:col + NS], xt, start=True, stop=True)
                last.then_inc(bc_ready, 1)

            def gv(q):
                h = q % NH
                tile = q // NH
                if q:
                    pe.wait_ge(gm_done, q)
                    pe.wait_ge(vt_done, q)
                if h == 0 and tile:
                    pe.wait_ge(row_done, tile)
                pe.wait_ge(sq_done, q + 1)
                for i in range(2):
                    pe.matmul(VT[32 * h:32 * h + 1, 2 * TS:4 * TS], ones[:], sq[q % 2][:, 2 * i:2 * i + 2, :],
                              start=(i == 0), stop=(i == 1))
                pe.wait_ge(wv_done, q + 1)
                v, w = vt[q % 2], wt[q % 8]
                for i in range(2):
                    pe.matmul(GG[:, 0:TS], v[:, i, :], w[:, i, :], start=(i == 0), stop=(i == 1))
                for i in range(2):
                    last = pe.transpose(VT[:, TS * i:TS * (1 + i)], v[:, i, :], ident[:])
                last.then_inc(gv_done, 1)

            def norms_back(tile):
                pe.wait_ge(row_done, tile + 1)
                hb = h_bank()
                pe.transpose(hb[:, 0:TS], rrow[:, 0, :], ident[:])
                for i in range(2):
                    last = pe.matmul(hb[:, (1 + i) * TS:(2 + i) * TS], rowsel[:, i, :], rrow[:, 1, :],
                                     start=True, stop=True)
                last.then_inc(h_ready, 1)

            def tail(tile):
                pe.wait_ge(ub_done, tile + 1)
                pe.wait_ge(vt_done, NH * (tile + 1))
                if tile:
                    pe.wait_ge(z_done, tile)
                    pe.wait_ge(acc, GT * NX * (tile // GT))
                u = ub[tile % 2]
                head = lambda h: slice(h * HD, (h + 1) * HD)
                rows = lambda h: slice((h % 2) * HD, (h % 2 + 1) * HD)
                for h in range(NH):
                    last = pe.matmul(RR[rows(h), (h // 2) * 2 * NS:(h // 2 + 1) * 2 * NS], u[:, head(h)],
                                     vts[(NH * tile + h) % 8], start=True, stop=True)
                last.then_inc(r_done, 1)
                pe.wait_ge(gm_done, NH * (tile + 1))
                pe.wait_ge(xi_done, tile + 1)
                if tile:
                    pe.wait_ge(x2_done, tile)
                for h0 in range(0, NH, 2):
                    for j in range(3):
                        for h in (h0, h0 + 1):
                            q = NH * tile + h
                            o = OO[rows(h), (h // 2) * TS:(h // 2 + 1) * TS]
                            if j == 0:
                                pe.matmul(o, u[:, head(h)], gts[q % 8][:], start=True, stop=False)
                            else:
                                last = pe.matmul(o, xi[tile % 2][:, j - 1, head(h)], wt[q % 8][:, j - 1, :],
                                                 start=False, stop=(j == 2))
                last.then_inc(tail_done, 1)

            def tail_T(tile):
                pe.wait_ge(rts_done, tile + 1)
                for i in range(2):
                    for j in range(2):
                        last = pe.transpose(RR[:, i * DI + j * 128:i * DI + (j + 1) * 128], rts[:, j, i, :], ident[:])
                last.then_inc(rt_done, 1)

            def op(tile):
                pe.wait_ge(y3_done, tile + 1)
                for i in range(2):
                    last = pe.matmul(OO[:, 0:DM], y3[tile % 2][:, i, :], woT[:, i, :], start=(i == 0), stop=(i == 1))
                last.then_inc(op_done, 1)

            def front(g):
                norm_T(LN1, g)
                front_dt(g)
                front_bcast(g)
                front_uz(g)

            pe.wait_ge(cst_g, 1)
            pe.wait_ge(ld_w, LD_W)
            front(0)
            pe.wait_ge(ld_f, LD_F)
            for g in range(NG):
                for k in range(KP):
                    q = KP * g + k
                    tile = q // NH
                    proj(q)
                    if k:
                        gv(q - 1)
                    if k >= NH:
                        if k % NH == 0 and k >= 2 * NH:
                            op(tile - 2)
                        if k % NH == 1:
                            norms_back(tile - 1)
                        if k % NH == 2:
                            tail(tile - 1)
                        if k % NH == 3:
                            tail_T(tile - 1)
                last_tile = GT * (g + 1) - 1
                gv(KP * (g + 1) - 1)
                op(last_tile - 1)
                norms_back(last_tile)
                tail(last_tile)
                tail_T(last_tile)
                op(last_tile)
                if g + 1 < NG:
                    front(g + 1)
                norm_T(LN2, g)
                router(g)
                router_T(g)
                for e in range(NX):
                    hidden(g, e)
                    if e:
                        expert_out(g, e - 1)
                expert_out(g, NE)

        @block.scalar
        def _(act):
            uses = [0]

            def h_read():
                n = uses[0]
                uses[0] += 1
                act.wait_ge(h_ready, n + 1)
                return HB[n % 2]

            def front(g):
                hb = h_read()
                xt = xnT
                if g:
                    act.wait_ge(h_free, uses[0] - 1)
                    act.activation(xt[:, 0:HALO], xt[:, GC:GC + HALO], ACT.Copy).then_inc(halo, 1)
                    act.wait_ge(halo, g)
                act.activation(xt[:, HALO:HALO + GC], hb[:], ACT.Copy).then_inc(h_free, 1)
                hb = h_read()
                act.activation(lraw[:], hb[:, 0:KP], ACT.Copy).then_inc(h_free, 1)
                act.wait_ge(dt_e, g + 1)
                act.activation(le[:], lx[:], ACT.Exp).then_inc(dt_exp, 1)
                hb = h_read()
                act.activation(dtr[:], hb[0:KP, 0:TS], ACT.Copy).then_inc(h_free, 1)
                if g:
                    act.wait_ge(step, STEP_OPS * g)
                for h in range(NH):
                    hb = h_read()
                    if g or h:
                        act.wait_ge(den_done, NH * g + h)
                    act.activation(sqn[:], hb[:].rearrange("p (c t) -> p c t", c=GT), ACT.Square,
                                   scale=theta[:, h:h + 1])
                    act.activation(view(ab, DTN + h * SL, (NH * SL, GT), (1, TS)),
                                   hb[:].rearrange("p (c t) -> p c t", c=GT), ACT.Copy).then_inc(h_free, 1)
                act.wait_ge(den_done, NH * (g + 1))
                act.activation(lden[:], lden[:], ACT.Ln, bias=1.0).then_inc(ln_den, 1)
                act.wait_ge(lcum, g + 1)
                act.activation(de[:, 0:PC], lden[:], ACT.Exp)
                act.activation(de[:, PC:2 * PC], lden[:], ACT.Exp, scale=-1.0).then_inc(de_done, 1)
                if g:
                    act.wait_ge(ub_done, GT * g)
                    act.wait_ge(y3_done, GT * g)
                for c2 in range(GT // 2):
                    hb = h_read()
                    last = act.activation(us[:, 2 * c2:2 * c2 + 2, :], hb[:].rearrange("p (c d) -> p c d", c=2), ACT.Silu)
                    last.then_inc(h_free, 1)
                for i in range(2):
                    hb = h_read()
                    act.activation(szT[:, i, :], hb[:], ACT.Silu).then_inc(h_free, 1)
                for i in range(2):
                    hb = h_read()
                    act.activation(uT[:, i, :], hb[:], ACT.Copy).then_inc(h_free, 1)

            def pair(q):
                act.wait_ge(bc_ready, q + 1)
                if q >= 2:
                    act.wait_ge(mul_done, q - 1)
                if q % KP == 0:
                    act.wait_ge(mat_p, q // KP + 1)
                b = BC[q % 2]
                act.activation(yc[q % 2][:], b[:].rearrange("p (j t) -> p j t", j=4), ACT.Copy)\
                    .then_inc(yc_done, 1)
                if q >= 2:
                    act.wait_ge(gv_done, q - 1)
                act.activation(sq[q % 2], b[:].rearrange("p (j t) -> p j t", j=4), ACT.Square).then_inc(sq_done, 1)

            def vt_copy(q):
                act.wait_ge(gv_done, q + 1)
                if q >= 8:
                    act.wait_ge(tail_done, (q - 8) // NH + 1)
                act.activation(vts[q % 8][:], VT[:, 0:2 * TS].rearrange("p (i n) -> p i n", i=2), ACT.Copy)\
                    .then_inc(vt_done, 1)
                if q % NH == NH - 1:
                    tile = q // NH
                    act.activation(rlog[:], VT[:, 2 * TS:4 * TS].rearrange("p (j t) -> p j t", j=2), ACT.Ln,
                                   bias=eps_l2[:]).then_inc(row_log, 1)
                    act.wait_ge(row_log, tile + 1)
                    if tile:
                        act.wait_ge(h_free, uses[0])
                    act.activation(rrow[:], rlog[:], ACT.Exp, scale=-0.5).then_inc(row_done, 1)

            def norms_copy(tile):
                hb = h_read()
                if tile:
                    act.wait_ge(gate_done, tile)
                act.activation(rbt[:], view(hb, 0, (32, NH)), ACT.Copy)
                act.activation(rcb[:], hb[:, TS:3 * TS].rearrange("p (i t) -> p i t", i=2), ACT.Copy)\
                    .then_inc(h_free, 1)

            def rts_copy(tile):
                act.wait_ge(r_done, tile + 1)
                if tile:
                    act.wait_ge(rt_done, tile)
                act.activation(rts[:], RR[:].rearrange("p (j i n) -> p j i n", j=2, i=2), ACT.Copy)\
                    .then_inc(rts_done, 1)

            def norm2(g):
                hb = h_read()
                if g:
                    act.wait_ge(y_ready, NX * g)
                act.activation(xnT2[:], hb[:], ACT.Copy).then_inc(h_free, 1)

            def router(g):
                hb = h_read()
                act.activation(lg[:], hb[:, 0:GT * NE].rearrange("p (c e) -> p c e", c=GT), ACT.Copy)\
                    .then_inc(h_free, 1)
                act.wait_ge(lg_c, g + 1)
                act.activation(el[:], ls[:], ACT.Exp).then_inc(el_done, 1)
                hb = h_read()
                act.activation(w9T[:], hb[0:NX, :], ACT.Copy).then_inc(h_free, 1)

            def gelus(g, e):
                n = g * NX + e
                for i in range(2):
                    hb = h_read()
                    if i == 0 and n >= 2:
                        act.wait_ge(y_ready, n - 1)
                    act.activation(hh[n % 2][:, i, :], hb[:], ACT.Gelu, bias=b1[:, e, i:i + 1]).then_inc(h_free, 1)

            act.wait_ge(ld_w, LD_W)
            act.activation(sgt[:, 2 * NH:4 * NH], sgt[:, 0:2 * NH], ACT.Exp, scale=-1.0).then_inc(prep_a, 1)
            act.wait_ge(cst_g, 1)
            act.wait_ge(prep, 1)
            front(0)
            for g in range(NG):
                for k in range(KP):
                    q = KP * g + k
                    tile = q // NH
                    pair(q)
                    if k:
                        vt_copy(q - 1)
                    if k >= NH:
                        if k % NH == 1:
                            norms_copy(tile - 1)
                        if k % NH == 2:
                            rts_copy(tile - 1)
                last_tile = GT * (g + 1) - 1
                vt_copy(KP * (g + 1) - 1)
                norms_copy(last_tile)
                rts_copy(last_tile)
                if g + 1 < NG:
                    front(g + 1)
                norm2(g)
                router(g)
                for e in range(NX):
                    gelus(g, e)

        @block.vector
        def _(dve):
            chain = [0]

            def link(ins):
                chain[0] += 1
                ins.then_inc(dve_chain, 1)
                dve.wait_ge(dve_chain, chain[0])

            def norm(kind, g):
                xg = xr[g % 3]
                if kind == LN1:
                    dve.wait_ge(ld_x[g], 16)
                for c in range(GT):
                    last = dve.bn_stats(stats[:, c, :], xg[:, c, :])
                link(last)
                for c in range(GT):
                    last = dve.bn_aggr(mv[:, c, :], stats[:, c, :])
                link(last)
                n = ln_index(kind, g)
                dve.tensor_scalar(mv[:, :, 1], mv[:, :, 1], EPS_LN, None, ALU.add).then_inc(ln_var, 1)
                dve.wait_ge(ln_rstd, n + 1)
                if n:
                    dve.wait_ge(h_ready, T_USE[n - 1])
                for c in range(GT):
                    last = dve.tensor_scalar(xn[:, c, :], xg[:, c, :], mv[:, c, 0:1], rstd[:, c:c + 1],
                                             ALU.subtract, ALU.mult)
                last.then_inc(ln_xn, 1)

            def front_dt(g):
                dve.wait_ge(h_free, F_USE[g] + 2)
                link(dve.tensor_tensor(lx[:].rearrange("p (c h) -> p c h", c=GT),
                                       lraw[:].rearrange("p (c h) -> p c h", c=GT),
                                       view(dtbb, 0, (0, GT), (1, NH)), ALU.add))
                dve.tensor_scalar(lx[:], lx[:], 0.0, None, ALU.min).then_inc(dt_e, 1)
                dve.wait_ge(dt_exp, g + 1)
                link(dve.tensor_scalar(le[:], le[:], E_MAX, None, ALU.min))
                link(dve.tensor_scalar(lp[0][:], le[:], 1.0 / 9, None, ALU.mult))
                for i, m in enumerate(range(8, 0, -1)):
                    c = (1.0 if m % 2 else -1.0) / m
                    link(dve.scalar_tensor_tensor(out=lp[(i + 1) % 2][:], in0=lp[i % 2][:], scalar=c, in1=le[:],
                                                  op0=ALU.add, op1=ALU.mult))
                if g:
                    dve.wait_ge(ub_done, GT * g)
                dve.tensor_scalar(dtt[:], lp[0][:], DT_MIN, DT_MAX, ALU.max, ALU.min).then_inc(dt_done, 1)

            def front_coef(g):
                dve.memset(view(lden, 0, (SL, KP), (1, 1)), 0.0)
                for h in range(NH):
                    dve.wait_ge(h_free, F_USE[g] + 4 + h)
                    dve.scalar_tensor_tensor(out=view(lden, h * SL + 1, (NH * SL, GT), (1, TS)),
                                             in0=view(ab, DTN + h * SL, (NH * SL, GT), (1, TS)), scalar=kvec[:, h:h + 1],
                                             in1=sqn[:], op0=ALU.mult, op1=ALU.add).then_inc(den_done, 1)
                dve.wait_ge(ln_den, g + 1)
                for k in range(KP):
                    last = dve.tensor_tensor_scan(ab[:, LCS + k * SL:LCS + (k + 1) * SL],
                                                  ones[:].broadcast_to([128, SL]), lden[:, k * SL:(k + 1) * SL],
                                                  0.0, ALU.mult, ALU.add)
                link(last)
                dve.tensor_tensor(view(lden, 0, (SL, KP), (1, SL)), view(ab, LCS, (SL, KP), (1, SL)),
                                  view(ab, LCS + MID, (SL, KP), (0, SL)), ALU.subtract).then_inc(lcum, 1)
                dve.wait_ge(de_done, g + 1)
                d = de
                link(dve.tensor_tensor(view(ab, PC + 1, (SL, KP), (1, TS)), view(d, PC + 1, (SL, KP), (1, TS)),
                                       view(ab, DTN, (SL, KP), (1, TS)), ALU.mult))
                for h in range(NH):
                    last = dve.scalar_tensor_tensor(out=view(ab, h * SL + 1, (NH * SL, GT), (1, TS)),
                                             in0=view(d, h * SL, (NH * SL, GT), (1, TS)), scalar=avec[:, h:h + 1],
                                             in1=view(ab, DTN + h * SL, (NH * SL, GT), (1, TS)),
                                                   op0=ALU.mult, op1=ALU.mult)
                last.then_inc(ab_done, 1)

            Y0, W0 = 0, 2 * PC
            issued = [0]

            def step_op(*args):
                dve.wait_ge(step, issued[0] - 1)
                dve.tensor_tensor(*args).then_inc(step, 1)
                issued[0] += 1

            def step_start(g):
                if g:
                    dve.wait_ge(wv_done, KP * g)
                dve.memset(view(pr, MID, (3 * PC, 2), (SL, KP)), 1.0)
                dve.memset(view(pr, PC + MID, (PC, 2), (SL, KP)), 0.0).then_inc(step, 1)
                issued[0] += 1
                dve.wait_ge(step, issued[0])

            def matrices(g):
                dve.wait_ge(ab_done, g + 1)
                for f in range(2):
                    dve.tensor_tensor(scr(f, 0), c1(f, 0), c2(f, 0), ALU.mult).then_inc(mat_d, 1)
                base = 10 * g

                def after(n):
                    dve.wait_ge(mat_d, base + n)

                for f in range(2):
                    after(1 + f)
                    dve.tensor_scalar(scr(f, 1), scr(f, 0), -1.0, 1.0, ALU.mult, ALU.add).then_inc(mat_d, 1)
                for f in range(2):
                    after(3 + f)
                    dve.tensor_tensor(scr(f, 0), c1(f, 1), scr(f, 1), ALU.mult).then_inc(mat_d, 1)
                for f in range(2):
                    after(5 + f)
                    dve.scalar_tensor_tensor(out=entry(f, "x", "v"), in0=scr(f, 0), scalar=-1.0, in1=c1(f, 0),
                                             op0=ALU.mult, op1=ALU.subtract).then_inc(mat_d, 1)
                for f in range(2):
                    after(7 + f)
                    dve.tensor_tensor(scr(f, 0), c2(f, 1), entry(f, "x", "v"), ALU.mult).then_inc(mat_d, 1)
                for f in range(2):
                    after(9 + f)
                    dve.tensor_tensor(entry(f, "v", "v"), scr(f, 1), scr(f, 0), ALU.add).then_inc(mat_e, 1)
                dve.wait_ge(mat_e, 2 * (g + 1))
                dve.wait_ge(mat_p, g + 1)

            def double_step(i):
                for t, operand in ((ta, 0), (tb, 1)):
                    for f in range(2):
                        slot = MID + (2 * i if f else -2 * i)
                        step_op(view(t[f], 0, (2 * KP, 2), (KP, 2), (1, KP)),
                                view(big, ((2 * f + operand) * 2) * DS * KP + i * KP, (DS * KP, 2), (0, 2), (1, KP)),
                                view(pr, operand * W0 + slot, (0, 2), (PC, 2), (SL, KP)), ALU.mult)
                for f in range(2):
                    slot = MID + (2 * i + 2 if f else -2 * i - 2)
                    step_op(view(pr, slot, (W0, 2), (PC, 2), (SL, KP)),
                            view(ta[f], 0, (2 * KP, 2), (KP, 2), (1, KP)),
                            view(tb[f], 0, (2 * KP, 2), (KP, 2), (1, KP)), ALU.add)

            filled = [0]

            def fill_tile(tile):
                o = (tile % GT) * NH * SL

                def fill_op(*args):
                    if filled[0] >= 2:
                        dve.wait_ge(fill, filled[0] - 1)
                    dve.tensor_tensor(*args).then_inc(fill, 1)
                    filled[0] += 1

                row = lambda f, comp, out: view(pr, comp * W0 + o + MID + (out if f else -out),
                                                (PC, 2), (SL, NH), (2 if f else -2, DS))
                coef = lambda f, kind: view(ab, kind * PC + o + (MID + 1 if f else MID),
                                            (0, 2), (SL, NH), (2 if f else -2, DS))
                tmp = lambda f: view(tf[f], 0, (NH * DS, 2), (DS, NH), (1, DS))
                for f in range(2):
                    fill_op(tmp(f), coef(f, 1 - f), row(f, 1 - f, 0), ALU.mult)
                for f in range(2):
                    fill_op(row(f, f, 1), row(f, f, 0), tmp(f), ALU.subtract)
                for f in range(2):
                    fill_op(tmp(f), coef(f, f), row(f, f, 1), ALU.mult)
                for f in range(2):
                    fill_op(row(f, 1 - f, 1), row(f, 1 - f, 0), tmp(f), ALU.add)

            def pair(q):
                g, k = divmod(q, KP)
                p, d = pr, de
                o = k * SL
                dve.wait_ge(yc_done, q + 1)
                dve.tensor_tensor(vc[q % 2][:], yc[q % 2][:, 2:4, :],
                                  view(d, o, (PC + 1, 2), (1, TS)), ALU.mult).then_inc(vc_done, 1)
                if q >= 2:
                    dve.wait_ge(wv_done, q - 1)
                m, y, v = mm[q % 2], yc[q % 2], vc[q % 2]
                over = lambda t, i: view(t, i * TS, (0, 2), (1, TS))
                dve.tensor_tensor(m[:, 0], over(y, 1), view(p, o + 1, (PC, 2), (1, TS)), ALU.mult)
                dve.tensor_tensor(m[:, 2], over(y, 0), view(p, W0 + o + 1, (PC, 2), (1, TS)), ALU.mult)
                dve.wait_ge(vc_done, q + 1)
                dve.tensor_tensor(m[:, 1], over(v, 1), view(p, W0 + o + 1, (PC, 2), (1, TS)), ALU.mult)
                dve.tensor_tensor(m[:, 3], over(v, 0), view(p, o, (PC, 2), (1, TS)), ALU.mult).then_inc(mul_done, 1)

            def gmask(q):
                dve.wait_ge(gv_done, q + 1)
                if q >= 8:
                    dve.wait_ge(tail_done, (q - 8) // NH + 1)
                dve.tensor_tensor(gts[q % 8], GG[:, 0:TS], causal[:], ALU.mult).then_inc(gm_done, 1)

            def state_sum(tile):
                dve.wait_ge(rt_done, tile + 1)
                if tile:
                    dve.wait_ge(xi_done, tile + 1)
                dve.tensor_tensor(zz[:], xi[tile % 2][:], RR[:].rearrange("p (i d) -> p i d", i=2), ALU.add)\
                    .then_inc(z_done, 1)

            def tile_out(tile):
                dve.wait_ge(tail_done, tile + 1)
                dve.wait_ge(gate_done, tile + 1)
                if tile >= 2:
                    dve.wait_ge(y3_done, tile - 1)
                dve.tensor_tensor(y1[tile % 2][:], OO[:, 0:2 * TS].rearrange("p (i t) -> p i t", i=2),
                                  gate[tile % 2][:], ALU.mult).then_inc(y1_done, 1)

            def skip_gate(g):
                dve.wait_ge(h_free, F_USE[g] + FRONT_USES)
                for i in range(2):
                    last = dve.scalar_tensor_tensor(out=uT[:, i, :], in0=uT[:, i, :], scalar=skipT[:, i:i + 1],
                                                    in1=szT[:, i, :], op0=ALU.mult, op1=ALU.mult)
                last.then_inc(skip_done, 1)

            def residual(tile):
                dve.wait_ge(op_done, tile + 1)
                xg = xr[(tile // GT) % 3][:, tile % GT, :]
                dve.tensor_tensor(xg, OO[:, 0:DM], xg, ALU.add).then_inc(x2_done, 1)

            def router(g):
                dve.wait_ge(h_free, R_USE[g] + 2)
                link(dve.tensor_reduce(lm[:], lg[:], AX.X, ALU.max))
                dve.tensor_tensor(ls[:], lg[:], view(lm, 0, (1, GT), (0, NE)), ALU.subtract).then_inc(lg_c, 1)
                lj = view(lg, 0, (NE, GT), (0, NE), (1, NE))
                li = view(lg, 0, (NE, GT), (1, NE), (0, NE))
                dve.tensor_tensor(cmp, lj, li, ALU.is_gt)
                link(dve.tensor_tensor(tie, lj, li, ALU.is_equal))
                flat = lambda t: t.rearrange("p c e j -> p c (e j)")
                link(dve.tensor_tensor(flat(tie), flat(tie), view(before, 0, (0, GT), (1, NE * NE)), ALU.mult))
                link(dve.tensor_tensor(cmp, cmp, tie, ALU.add))
                link(dve.tensor_reduce(rank[:], cmp, AX.X, ALU.add))
                dve.wait_ge(el_done, g + 1)
                link(dve.tensor_reduce(esum[:], el[:], AX.X, ALU.add))
                link(dve.reciprocal(einv[:], esum[:]))
                link(dve.scalar_tensor_tensor(out=selw[:], in0=rank[:], scalar=1.5, in1=el[:],
                                              op0=ALU.is_lt, op1=ALU.mult))
                if g:
                    dve.wait_ge(acc, GT * NX * g)
                dve.memset(w9[:, :, NE:NX], 1.0)
                dve.tensor_tensor(w9[:, :, 0:NE], selw[:], view(einv, 0, (1, GT), (0, NE)), ALU.mult)\
                    .then_inc(w9_done, 1)

            def add_expert(g, e):
                n = g * NX + e
                dve.wait_ge(y_ready, n + 1)
                yb = YY[n % 2]
                for c in range(GT):
                    if e:
                        dve.wait_ge(acc, GT * (n - 1) + c + 1)
                    xg = xr[g % 3][:, c, :]
                    dve.scalar_tensor_tensor(out=xg, in0=yb[:, c * TS:(c + 1) * TS], scalar=w9[:, c, e:e + 1],
                                             in1=xg, op0=ALU.mult, op1=ALU.add).then_inc(acc, 1)

            dve.wait_ge(ld_w, LD_W)
            dve.memset(ones[:], 1.0)
            dve.memset(onesrow[:], 1.0)
            dve.memset(mhalf[:], -0.5)
            dve.memset(eps_l2[:], EPS_L2)
            dve.memset(xnT[:, 0:HALO], 0.0)
            dve.memset(VT[:], 1.0)
            dve.memset(lden[:], 0.0).then_inc(cst, 1)
            dve.wait_ge(cst, 1)
            dve.wait_ge(prep_a, 1)
            link(dve.tensor_scalar(sgt[:, 2 * NH:], sgt[:, 2 * NH:], 1.0, None, ALU.add))
            link(dve.reciprocal(sgt[:, 2 * NH:], sgt[:, 2 * NH:]))
            dve.tensor_scalar(kvec[:], sgt[:, 3 * NH:], K_MAX, None, ALU.mult)
            link(dve.tensor_scalar(theta[:], sgt[:, 2 * NH:3 * NH], PI, None, ALU.mult))
            dve.tensor_tensor(avec[:], theta[:], theta[:], ALU.mult).then_inc(prep, 1)
            dve.wait_ge(prep, 1)
            norm(LN1, 0)
            for k in range(TAPS):
                last = dve.tensor_tensor(taps[:, k, :], taps[:, k, :], winT[:, COL_U:COL_U + DI], ALU.mult)
            last.then_inc(taps_done, 1)
            front_dt(0)
            front_coef(0)
            for g in range(NG):
                matrices(g)
                step_start(g)
                for i in range(DS):
                    double_step(i)
                    if g and i % EXPERT_EVERY == EXPERT_EVERY - 1 and i // EXPERT_EVERY < NX:
                        add_expert(g - 1, i // EXPERT_EVERY)
                dve.wait_ge(step, STEP_OPS * (g + 1))
                skip_gate(g)
                for k in range(KP):
                    q = KP * g + k
                    tile = q // NH
                    if k % NH == 0:
                        fill_tile(tile)
                        dve.wait_ge(fill, 8 * (tile + 1))
                    pair(q)
                    if k:
                        gmask(q - 1)
                    if k >= NH:
                        if k % NH == 0 and k >= 2 * NH:
                            state_sum(tile - 2)
                        if k % NH == 1 and k >= 2 * NH:
                            residual(tile - 2)
                        if k % NH == 3:
                            tile_out(tile - 1)
                last_tile = GT * (g + 1) - 1
                gmask(KP * (g + 1) - 1)
                state_sum(last_tile - 1)
                residual(last_tile - 1)
                tile_out(last_tile)
                state_sum(last_tile)
                residual(last_tile)
                dve.wait_ge(x2_done, last_tile + 1)
                if g + 1 < NG:
                    norm(LN1, g + 1)
                    front_dt(g + 1)
                    front_coef(g + 1)
                norm(LN2, g)
                router(g)
            for e in range(NX):
                add_expert(NG - 1, e)

        @block.gpsimd
        def _(pool):
            chain = [0]

            def link(ins):
                chain[0] += 1
                ins.then_inc(pool_chain, 1)
                pool.wait_ge(pool_chain, chain[0])

            def rstd_of(n):
                pool.wait_ge(ln_var, n + 1)
                if n:
                    pool.wait_ge(ln_xn, n)
                pool.tensor_tensor(rstd[:], mv[:, :, 1], mhalf[:, 0:GT], ALU.pow).then_inc(ln_rstd, 1)

            def crossings(g):
                pool.wait_ge(step, STEP_OPS * (g + 1))
                p, d = pr, de
                W0 = 2 * PC
                if g:
                    link(pool.tensor_copy(edge[:, :, 0:NH], edge[:, :, KP:KP + NH]))
                pool.tensor_copy(edge[:, 0:2, NH:], view(p, TS, (PC, 2), (SL, KP)))
                link(pool.tensor_tensor(edge[:, 2:4, NH:], view(p, W0 + TS, (PC, 2), (SL, KP)),
                                        view(d, PC + TS, (0, 2), (SL, KP)), ALU.mult))
                link(pool.tensor_tensor(ew[:], edge[:, 2:4, 0:KP], view(d, 0, (0, 2), (SL, KP)), ALU.mult))
                first = lambda o: view(p, o, (0, 2), (SL, KP))
                y = edge[:, 0:2, 0:KP]
                pool.tensor_tensor(tra[:, 0], first(W0 + PC), y, ALU.mult)
                pool.tensor_tensor(tra[:, 1], first(PC), ew[:], ALU.mult)
                pool.tensor_tensor(tra[:, 2], first(0), ew[:], ALU.mult)
                link(pool.tensor_tensor(tra[:, 3], first(W0), y, ALU.mult))
                pool.tensor_tensor(tr[:, :, 0, :], tra[:, 0], tra[:, 1], ALU.subtract)
                link(pool.tensor_tensor(tr[:, :, 1, :], tra[:, 2], tra[:, 3], ALU.subtract))

            def wv(q):
                pool.wait_ge(mul_done, q + 1)
                if q >= 8:
                    pool.wait_ge(tail_done, (q - 8) // NH + 1)
                m = mm[q % 2]
                pool.tensor_tensor(wt[q % 8][:], m[:, 0], m[:, 1], ALU.add)
                if q >= 2:
                    pool.wait_ge(gv_done, q - 1)
                pool.tensor_tensor(vt[q % 2][:, 0, :], m[:, 2, 1, :], m[:, 3, 1, :], ALU.subtract)
                pool.tensor_tensor(vt[q % 2][:, 1, :], m[:, 3, 0, :], m[:, 2, 0, :], ALU.subtract).then_inc(wv_done, 1)

            def matrices(g):
                pool.wait_ge(ab_done, g + 1)
                for f in range(2):
                    last = pool.tensor_tensor(scr_p(f), c1(f, 1), c2(f, 0), ALU.mult)
                link(last)
                for f in range(2):
                    last = pool.tensor_scalar(entry(f, "x", "x"), scr_p(f), -1.0, 1.0, ALU.mult, ALU.add)
                link(last)
                for f in range(2):
                    last = pool.tensor_tensor(scr_p(f), c2(f, 1), entry(f, "x", "x"), ALU.mult)
                link(last)
                for f in range(2):
                    last = pool.tensor_tensor(entry(f, "v", "x"), c2(f, 0), scr_p(f), ALU.add)
                last.then_inc(mat_p, 1)

            def ubar(tile):
                g, c = divmod(tile, GT)
                pool.wait_ge(h_free, M_USE[g] + c + 1)
                link(pool.tensor_tensor(du[:], rbt[:], dtt[:, NH * c:NH * c + NH], ALU.mult))
                if tile >= 2:
                    pool.wait_ge(tail_done, tile - 1)
                    pool.wait_ge(y1_done, tile - 1)
                pool.tensor_tensor(ub[tile % 2][:].rearrange("p (h d) -> p h d", h=NH),
                                   us[:, c, :].rearrange("p (h d) -> p h d", h=NH),
                                   view(du, 0, (1, NH), (0, HD)), ALU.mult).then_inc(ub_done, 1)
                pool.tensor_tensor(gate[tile % 2][:], rcb[:], szT[:, :, c * TS:(c + 1) * TS], ALU.mult)\
                    .then_inc(gate_done, 1)

            def add_skip(tile):
                g, c = divmod(tile, GT)
                pool.wait_ge(y1_done, tile + 1)
                pool.wait_ge(skip_done, g + 1)
                if tile >= 2:
                    pool.wait_ge(op_done, tile - 1)
                pool.tensor_tensor(y3[tile % 2][:], y1[tile % 2][:], uT[:, :, c * TS:(c + 1) * TS], ALU.add)\
                    .then_inc(y3_done, 1)

            def state(tile):
                k = NH * (tile % GT)
                pool.wait_ge(z_done, tile)
                pick = lambda col: view(tr, col * 2 * KP + k, (KP, 2), (1, NH), (0, HD))
                full = lambda t: t[:].rearrange("p i (h d) -> p i h d", h=NH)
                pool.tensor_tensor(full(x1), pick(0), view(zz, 0, (0, 2), (HD, NH), (1, HD)), ALU.mult)
                link(pool.tensor_tensor(full(x2), pick(1), view(zz, DI, (0, 2), (HD, NH), (1, HD)), ALU.mult))
                pool.tensor_tensor(xi[tile % 2][:], x1[:], x2[:], ALU.add).then_inc(xi_done, 1)

            pool.memset(xi[0][:], 0.0).then_inc(xi_done, 1)
            pool.memset(edge[:], 0.0)
            pool.memset(rowsel[:], 0.0)
            pool.memset(ident[:], 0.0)
            pool.memset(causal[:], 1.0)
            link(pool.memset(before[:], 1.0))
            pool.affine_select(out=rowsel[:].rearrange("p i (a d) -> p i a d", a=2),
                               in_=rowsel[:].rearrange("p i (a d) -> p i a d", a=2), compare_op=ALU.not_equal,
                               fill=1.0, base=0, pattern=[[-64, 2], [-32, 2], [0, HD]], channel_multiplier=1)
            pool.affine_select(out=ident[:], in_=ident[:], compare_op=ALU.not_equal, fill=1.0, base=0,
                               pattern=[[-1, 128]], channel_multiplier=1)
            pool.affine_select(out=causal[:], in_=causal[:], compare_op=ALU.is_ge, fill=0.0, base=0,
                               pattern=[[1, 128]], channel_multiplier=-1)
            link(pool.affine_select(out=before[:], in_=before[:], compare_op=ALU.is_gt, fill=0.0, base=0,
                                    pattern=[[1, NE], [-1, NE]], channel_multiplier=0))
            pool.wait_ge(cst, 1)
            pool.memset(ew[:], 0.0).then_inc(cst_g, 1)
            rstd_of(0)
            for g in range(NG):
                matrices(g)
                crossings(g)
                for k in range(KP):
                    q = KP * g + k
                    tile = q // NH
                    wv(q)
                    if k >= NH:
                        if k % NH == 0 and tile > 1:
                            state(tile - 1)
                        if k % NH == 1:
                            ubar(tile - 1)
                        if k % NH == 3:
                            add_skip(tile - 1)
                last_tile = GT * (g + 1) - 1
                state(last_tile)
                ubar(last_tile)
                add_skip(last_tile)
                if g + 1 < NG:
                    rstd_of(ln_index(LN1, g + 1))
                rstd_of(ln_index(LN2, g))


def kernel(**inputs):
    import numpy as np
    import concourse.bacc as bacc
    from concourse.bass_utils import run_bass_kernel_spmd

    a = {n.split("_", 1)[1]: np.asarray(v) for n, v in inputs.items()}
    hidden_cols = lambda v: v.reshape(-1, 2, 128).transpose(2, 0, 1)
    laid = {
        "x": a["attn_x"], "w_inT": a["attn_W_in"].T, "dw_wT": a["attn_dw_weight"].T, "dw_b": a["attn_dw_bias"],
        "w_outT": a["attn_W_out"].T, "skipT_in": a["attn_skip"].reshape(2, 128).T, "dt_bias": a["attn_dt_bias"],
        "theta_rawT": a["attn_theta_raw"].T, "k_rawT": a["attn_k_raw"].T,
        "router_w": a["ffn_router_w"], "router_b": a["ffn_router_b"],
        "sw1": a["ffn_sw1"], "sb1T": hidden_cols(a["ffn_sb1"])[:, 0], "sw2": a["ffn_sw2"], "sb2": a["ffn_sb2"],
        "rw1": a["ffn_rw1"], "rb1T": hidden_cols(a["ffn_rb1"]), "rw2": a["ffn_rw2"], "rb2": a["ffn_rb2"],
    }
    nc = bacc.Bacc("TRN2", target_bir_lowering=False, num_devices=1)
    arrays, args = {}, {}
    for name, v in laid.items():
        v = np.ascontiguousarray(v)
        arrays[f"in_{name}"] = v
        args[name] = nc.dram_tensor(f"in_{name}", v.shape, mybir.dt.from_np(v.dtype), kind="ExternalInput").ap()
    args["out"] = nc.dram_tensor("out_0", (1, T, DM), F32, kind="ExternalOutput").ap()
    build(nc, **args)
    r = run_bass_kernel_spmd(nc, [arrays], core_ids=[0])
    return r.results[0]["out_0"]
```

```python
from contextlib import ExitStack

import concourse.bass as bass
from concourse import mybir

F32 = mybir.dt.float32
ALU = mybir.AluOpType
ACT = mybir.ActivationFunctionType
AX = mybir.AxisListType

T, DM = 2048, 128
NH, HD, NS = 4, 64, 128
DI = NH * HD
TAPS = 4
NE, NX, HF = 8, 9, 256
TS = 128
GT = 4
NT, NG = T // TS, T // (TS * GT)
KP = GT * NH
GC = GT * TS
SL = TS + 1
MID = TS // 2
PC = KP * SL
DT_MIN, DT_MAX = 1e-4, 0.1
E_MAX = 0.11
PI = 3.141592653589793
K_MAX = 0.5
EPS_LN, EPS_L2 = 1e-5, 1e-8
HALO = TAPS - 1
COL_Z, COL_U, COL_DT, COL_BC = 0, DI, 2 * DI, 2 * DI + NH
DS = MID // 2
EXPERT_FIRST, EXPERT_EVERY = 5, 3
MAT_OPS = 14
ROUTER_STAGES = 8
STEP_OPS = 4 * DS + 1
FILLS = (8, 8, 8, 4)
FILL_LAST = DS - sum(FILLS)
FILL_OPS = 8 * len(FILLS)
PRODUCTS, NORMS, NORMS_C, TAIL, TAIL_T, OUT = 1, 2, 4, 4, 6, 7
G_COPY, MASK, UBAR, GATES, TILE_OUT, STATE_SUM, STATE = 2, 2, 3, 5, 6, 7, 3
MID_STEPS = KP + OUT + 1
L_U, L_Z, L_US = KP + 4, KP + 4, KP + 6
P_FIRST = (KP + 1, KP + 2)
F_INV, F_BETA, F_DEN, F_ALPHA = KP + 2, KP + 3, KP + 3, KP + 4
(F_STATS, F_XN, F_XNT, F_LOGITS, F_EXP, F_LOG1P, F_ROWS, F_BCAST, F_LOG, F_SCAN, F_CENTRE) = (
    1, 2, 3, 5, 6, 7, 8, 9, 13, 15, 17)


def due(g, k, lag):
    c, r = divmod(k - lag - (NH - 1), NH)
    return [GT * g + c] if r == 0 and 0 <= c < GT else []


def view(t, offset, *dims):
    full = t[:]
    return bass.AP(tensor=full.tensor, offset=full.offset + offset,
                   ap=[list(full.ap[0])] + [[s, n] for s, n in dims])


def build(nc, x, w_inT, dw_wT, dw_bT, w_outT, skipT_in, dt_bias, theta_rawT, k_rawT,
          router_w, router_b, sw1, sb1T, sw2, sb2, rw1, rb1T, rw2, rb2, out):
    ctx = ExitStack()
    with ctx:
        def sb(name, *shape, dtype=F32):
            return ctx.enter_context(nc.sbuf_tensor(name, list(shape), dtype))

        def sem(name):
            return ctx.enter_context(nc.semaphore(name))

        winT = sb("winT", DM, 2 * DI + NH + 4 * NH * NS)
        taps = sb("taps", DM, TAPS, DI)
        biasu = sb("biasu", 128, 2)
        woT = sb("woT", 128, 2, DM)
        skipT = sb("skipT", 128, 2)
        dtbb = sb("dtbb", 128, NH)
        theta = sb("theta", NS, NH)
        avec = sb("avec", NS, NH)
        kvec = sb("kvec", NS, NH)
        sgt = sb("sgt", NS, 4 * NH)
        rw = sb("rw", DM, NE)
        rb = sb("rb", 128, NE)
        w1 = sb("w1", DM, NX, HF)
        b1 = sb("b1", 128, NX, 2)
        w2 = sb("w2", 128, NX, 2, DM)
        b2 = sb("b2", NX, DM)
        ident = sb("ident", 128, 128)
        before = sb("before", 128, NE, NE)
        ones = sb("ones", 128, 1)
        eps_l2 = sb("eps_l2", 128, 1)
        mhalf = sb("mhalf", 128, 8)
        xr = [sb(f"xr{i}", 128, GT, DM) for i in range(3)]
        xn = sb("xn", 128, GT, DM)
        xnTs = [sb(f"xnT{i}", DM, HALO + GC) for i in range(2)]
        stats = sb("stats", 128, GT, 6)
        mv = sb("mv", 128, GT, 2)
        rstd = sb("rstd", 128, GT)
        lraw = sb("lraw", 128, KP)
        lx = sb("lx", 128, KP)
        le = sb("le", 128, KP)
        lp = [sb(f"lp{i}", 128, KP) for i in range(2)]
        dtts = [sb(f"dtt{i}", 128, KP) for i in range(2)]
        dtr = sb("dtr", KP, TS)
        lden = sb("lden", NS, PC)
        de = sb("de", NS, 2 * PC)
        ab = sb("ab", NS, 2 * PC)
        DTN, LCS = 1, PC
        szT = sb("szT", 128, 2, GC)
        uT = sb("uT", 128, 2, GC)
        us = sb("us", 128, GT, DI)
        pr = sb("pr", NS, 4 * PC)
        tp = [sb(f"tp{i}", NS, 8 * KP) for i in range(2)]
        tf = [sb(f"tf{i}", NS, 2 * KP * max(FILLS)) for i in range(2)]
        yc = [sb(f"yc{i}", NS, 4, TS) for i in range(2)]
        sqs = sb("sqs", NS, 2 * 4 * TS)
        sq = [sqs[:, i * 4 * TS:(i + 1) * 4 * TS].rearrange("p (j t) -> p j t", j=4)
              for i in range(2)]
        mm = [sb(f"mm{i}", NS, 4, 2, TS) for i in range(2)]
        big = sb("big", 128, 16 * 2 * TS)
        part = lambda i: big[:, i * 2 * TS:(i + 1) * 2 * TS].rearrange("p (i t) -> p i t", i=2)
        wt = [part(i) for i in range(8)]
        vt = [sb(f"vt{i}", NS, 2, TS) for i in range(2)]
        vts = [part(8 + i) for i in range(8)]
        gtm = sb("gtm", TS, 8 * TS)
        gts = [gtm[:, i * TS:(i + 1) * TS] for i in range(8)]
        rrow = sb("rrow", 128, 2, TS)
        nsq = sb("nsq", 128, 2, NH)
        rinv = sb("rinv", 128, 2, NH)
        rcb = sb("rcb", 128, 2, TS)
        gate = [sb(f"gate{i}", 128, 2, TS) for i in range(2)]
        rts = sb("rts", 128, 2, 2, NS)
        du = sb("du", 128, NH)
        ub = [sb(f"ub{i}", 128, DI) for i in range(2)]
        xi = [sb(f"xi{i}", NS, 2, DI) for i in range(2)]
        zz = sb("zz", NS, 2, DI)
        x1 = sb("x1", NS, 2, DI)
        x2 = sb("x2", NS, 2, DI)
        edge = sb("edge", NS, 4, NH + KP)
        ew = sb("ew", NS, 2, KP)
        tra = sb("tra", NS, 4, 2, KP)
        tr = sb("tr", NS, 2, 2, KP)
        y1 = [sb(f"y1{i}", 128, 2, TS) for i in range(2)]
        y3 = [sb(f"y3{i}", 128, 2, TS) for i in range(2)]
        xnT2 = sb("xnT2", DM, GC)
        lg = sb("lg", 128, GT, NE)
        lm = sb("lm", 128, GT)
        ls = sb("ls", 128, GT, NE)
        el = sb("el", 128, GT, NE)
        esum = sb("esum", 128, GT)
        einv = sb("einv", 128, GT)
        cmp, tie = (t[:].rearrange("p (c e j) -> p c e j", c=GT, e=NE) for t in tf)
        rank = sb("rank", 128, GT, NE)
        selw = sb("selw", 128, GT, NE)
        w9 = sb("w9", 128, GT, NX)
        w9T = sb("w9T", NX, GC)
        hh = [t[:].rearrange("p (i t) -> p i t", i=2) for t in (gtm, sqs)]

        def bank(name):
            return ctx.enter_context(nc.psum_tensor(name, [128, 512], F32))
        BC = [bank("BC0"), bank("BC1")]
        GG = bank("GG")
        VT = bank("VT")
        RR = bank("RR")
        OO = bank("OO")
        YY = [RR, OO]
        HB = [bank("HB0"), bank("HB1")]

        ld_x = [sem(f"ld_x{g}") for g in range(NG)]
        ld_s, ld_u, ld_w, ld_f, st_out = sem("ld_s"), sem("ld_u"), sem("ld_w"), sem("ld_f"), sem("st_out")
        cst, cst_g, prep, prep_a = sem("cst"), sem("cst_g"), sem("prep"), sem("prep_a")
        taps_done = sem("taps_done")
        ln_var, ln_rstd, ln_xn = sem("ln_var"), sem("ln_rstd"), sem("ln_xn")
        h_ready, h_free = sem("h_ready"), sem("h_free")
        dt_e, dt_exp, dt_done = sem("dt_e"), sem("dt_exp"), sem("dt_done")
        den_done, ln_den, lcum, de_done, ab_done = (sem(s) for s in
                                                    ("den_done", "ln_den", "lcum", "de_done", "ab_done"))
        skip_done = sem("skip_done")
        inv_done = sem("inv_done")
        tr_done, x_done = sem("tr_done"), sem("x_done")
        scan_done, inv_den, beta_done = sem("scan_done"), sem("inv_den"), sem("beta_done")
        mat_p, mat_d, mat_e, step, fill, fill_d = (sem(s) for s in
                                                      ("mat_p", "mat_d", "mat_e", "step", "fill", "fill_d"))
        bc_ready, yc_done, sq_done, vc_done, mul_done, wv_done = (sem(s) for s in
            ("bc_ready", "yc_done", "sq_done", "vc_done", "mul_done", "wv_done"))
        gv_done, gm_done, vt_done, row_done, ub_done, gate_done = (sem(s) for s in
            ("gv_done", "gm_done", "vt_done", "row_done", "ub_done", "gate_done"))
        r_done, tail_done, rts_done, rt_done, z_done, y1_done, y3_done, op_done, x2_done, xi_done = (sem(s) for s in
            ("r_done", "tail_done", "rts_done", "rt_done", "z_done", "y1_done", "y3_done", "op_done", "x2_done",
             "xi_done"))
        router_d, gc_done = sem("router_d"), sem("gc_done")
        lg_c, el_done, w9_done, y_ready, acc = (sem(s) for s in ("lg_c", "el_done", "w9_done", "y_ready", "acc"))
        dve_chain, pool_chain = sem("dve_chain"), sem("pool_chain")

        def coef2(f, kind, second):
            slot = MID + 1 + second if f else MID - second
            return view(ab, kind * PC + slot, (2 if f else -2, DS), (SL, KP))

        c1 = lambda f, second: coef2(f, 1 - f, second)
        c2 = lambda f, second: coef2(f, f, second)

        def entry(f, row, operand):
            comp = lambda role: f if role == "x" else 1 - f
            return view(big, ((2 * f + comp(operand)) * 2 + comp(row)) * DS * KP, (KP, DS), (1, KP))

        scr = lambda f, i: view(mm[f], i * DS * KP, (KP, DS), (1, KP))
        scr_x = lambda f: view(yc[f], 0, (KP, DS), (1, KP))

        def fill_slots(fill_op, scratch, i0, n):
            row = lambda f, comp, out: view(pr, comp * 2 * PC + (MID + 2 * i0 + out if f else MID - 2 * i0 - out),
                                            (PC, 2), (SL, KP), (2 if f else -2, n))
            coef = lambda f, kind: view(ab, kind * PC + (MID + 1 + 2 * i0 if f else MID - 2 * i0),
                                        (0, 2), (SL, KP), (2 if f else -2, n))
            tmp = lambda f: view(scratch[f], 0, (KP * n, 2), (n, KP), (1, n))
            for f in range(2):
                fill_op(tmp(f), coef(f, 1 - f), row(f, 1 - f, 0), ALU.mult)
            for f in range(2):
                fill_op(row(f, f, 1), row(f, f, 0), tmp(f), ALU.subtract)
            for f in range(2):
                fill_op(tmp(f), coef(f, f), row(f, f, 1), ALU.mult)
            for f in range(2):
                fill_op(row(f, 1 - f, 1), row(f, 1 - f, 0), tmp(f), ALU.add)

        block = ctx.enter_context(nc.Block())
        LN1, LN2 = 0, 1

        def ln_index(kind, g):
            if kind == LN1:
                return max(2 * g - 1, 0)
            return 2 * g + 2 if g < NG - 1 else 2 * g + 1

        USE = {}

        def plan(*name):
            USE[name] = len(USE)

        def plan_early(g, k):
            if k == F_XNT:
                plan("xnT", g)
            if k == F_LOGITS:
                plan("logits", g)
            if k == F_ROWS:
                plan("rows", g)
            if 0 <= k - F_BCAST < NH:
                plan("bcast", g, k - F_BCAST)

        for k in range(MID_STEPS):
            plan_early(0, k)
        for i in range(2):
            for what in ("u", "z", "us"):
                plan(what, 0, i)
        for g in range(NG):
            for k in range(MID_STEPS):
                for tile in due(g, k, NORMS):
                    plan("norms", tile)
                for tile in due(g, k, NORMS_C):
                    plan("normsC", tile)
                if g + 1 < NG:
                    plan_early(g + 1, k)
                    for what, at in (("u", L_U), ("z", L_Z), ("us", L_US)):
                        if k == at:
                            plan(what, g + 1, 0)
            if g + 1 < NG:
                plan("u", g + 1, 1)
                plan("z", g + 1, 1)
            plan("xnT2", g)
            plan("router", g)
            if g + 1 < NG:
                plan("us", g + 1, 1)
            for e in range(NX):
                if e == NE:
                    plan("w9T", g)
                plan("hidden", g, e, 0)
                plan("hidden", g, e, 1)
        h_read_of = lambda *name: USE[name] + 1

        @block.sync
        def _(sp):
            xv = x.rearrange("o (g c t) d -> (o g) t c d", g=NG, c=GT)
            ov = out.rearrange("o (g c t) d -> (o g) t c d", g=NG, c=GT)

            def dma_x(g):
                if g >= 3:
                    sp.wait_ge(st_out, 16 * (g - 2))
                sp.dma_start(xr[g % 3][:], xv[g]).then_inc(ld_x[g], 16)

            dma_x(0)
            sp.dma_start(winT[:, COL_U:COL_BC], w_inT[:, COL_U:COL_BC]).then_inc(ld_u, 16)
            sp.dma_start(sgt[:, 0:NH], theta_rawT).then_inc(ld_s, 16)
            sp.dma_start(sgt[:, NH:2 * NH], k_rawT).then_inc(ld_s, 16)
            sp.dma_start(dtbb[:], dt_bias.rearrange("(o h) -> o h", o=1).broadcast_to([128, NH])).then_inc(ld_s, 16)
            dw_row = dw_wT.rearrange("(o k) d -> o k d", o=1)
            sp.dma_start(taps[:], dw_row.broadcast_to([128, TAPS, DI])).then_inc(ld_u, 16)
            sp.dma_start(biasu[:], dw_bT).then_inc(ld_w, 16)
            sp.dma_start(skipT[:], skipT_in).then_inc(ld_w, 16)
            sp.dma_start(winT[:, 0:COL_U], w_inT[:, 0:COL_U]).then_inc(ld_w, 16)
            sp.dma_start(winT[:, COL_BC:], w_inT[:, COL_BC:]).then_inc(ld_w, 16)
            dma_x(1)
            dma_x(2)
            sp.dma_start(woT[:], w_outT.rearrange("(i d) m -> d i m", i=2)).then_inc(ld_f, 16)
            sp.dma_start(rw[:], router_w).then_inc(ld_f, 16)
            sp.dma_start(rb[:], router_b.rearrange("(o e) -> o e", o=1).broadcast_to([128, NE])).then_inc(ld_f, 16)
            sp.dma_start(w1[:, 0:NE, :], rw1.rearrange("e d h -> d e h")).then_inc(ld_f, 16)
            sp.dma_start(w1[:, NE, :], sw1).then_inc(ld_f, 16)
            sp.dma_start(b1[:, 0:NE, :], rb1T).then_inc(ld_f, 16)
            sp.dma_start(b1[:, NE, :], sb1T).then_inc(ld_f, 16)
            sp.dma_start(w2[:, 0:NE, :, :], rw2.rearrange("e (i h) d -> h e i d", i=2)).then_inc(ld_f, 16)
            sp.dma_start(w2[:, NE, :, :], sw2.rearrange("(i h) d -> h i d", i=2)).then_inc(ld_f, 16)
            sp.dma_start(b2[0:NE, :], rb2).then_inc(ld_f, 16)
            sp.dma_start(b2[NE:NX, :], sb2.rearrange("(o d) -> o d", o=1)).then_inc(ld_f, 16)
            for g in range(NG):
                sp.wait_ge(acc, GT * NX * (g + 1))
                sp.dma_start(ov[g], xr[g % 3][:]).then_inc(st_out, 16)
                if g + 3 < NG:
                    dma_x(g + 3)
            sp.wait_ge(st_out, 16 * NG)
        LD_S, LD_U, LD_W, LD_F = 3 * 16, 2 * 16, 4 * 16, 11 * 16

        @block.tensor
        def _(pe):
            uses = [0]

            def h_bank(*name):
                n = USE[name]
                assert n == uses[0]
                uses[0] += 1
                if n >= 2:
                    pe.wait_ge(h_free, n - 1)
                return HB[n % 2]

            def norm_T(kind, g):
                pe.wait_ge(ln_xn, ln_index(kind, g) + 1)
                hb = h_bank("xnT" if kind == LN1 else "xnT2", g)
                for c in range(GT):
                    last = pe.transpose(hb[:, c * TS:(c + 1) * TS], xn[:, c, :], ident[:])
                last.then_inc(h_ready, 1)

            def front_early(g, k):
                if k == F_XNT:
                    norm_T(LN1, g)
                if k == F_LOGITS:
                    pe.wait_ge(h_free, h_read_of("xnT", g))
                    hb = h_bank("logits", g)
                    for c in range(GT):
                        last = pe.matmul(hb[:, NH * c:NH * c + NH],
                                         xnTs[g % 2][:, HALO + c * TS:HALO + (c + 1) * TS],
                                         winT[:, COL_DT:COL_DT + NH], start=True, stop=True)
                    last.then_inc(h_ready, 1)
                if k == F_ROWS:
                    pe.wait_ge(dt_done, g + 1)
                    hb = h_bank("rows", g)
                    pe.transpose(hb[0:KP, 0:TS], dtts[g % 2][:], ident[:]).then_inc(h_ready, 1)
                if 0 <= k - F_BCAST < NH:
                    h = k - F_BCAST
                    pe.wait_ge(h_free, h_read_of("rows", g))
                    hb = h_bank("bcast", g, h)
                    for c in range(GT):
                        row = NH * c + h
                        last = pe.matmul(hb[:, c * TS:(c + 1) * TS], ident[0:KP, row:row + 1].broadcast_to([KP, 128]),
                                         dtr[:], start=True, stop=True)
                    last.then_inc(h_ready, 1)

            def front_late(g, what, i):
                if g == 0:
                    pe.wait_ge(taps_done, 1)
                xt = xnTs[g % 2]
                o = i * 2 * TS
                hb = h_bank(what, g, i)
                if what == "u":
                    for j in range(2):
                        for k in range(TAPS):
                            last = pe.matmul(hb[:, j * 2 * TS:(j + 1) * 2 * TS], taps[:, k, j * 128:(j + 1) * 128],
                                             xt[:, o + k:o + k + 2 * TS], start=(k == 0), stop=(k == TAPS - 1))
                if what == "z":
                    for j in range(2):
                        last = pe.matmul(hb[:, j * 2 * TS:(j + 1) * 2 * TS],
                                         winT[:, COL_Z + j * 128:COL_Z + (j + 1) * 128],
                                         xt[:, HALO + o:HALO + o + 2 * TS], start=True, stop=True)
                if what == "us":
                    pe.wait_ge(h_free, h_read_of("u", g, i))
                    for c in range(2):
                        for j in range(2):
                            last = pe.transpose(hb[:, c * DI + j * 128:c * DI + (j + 1) * 128],
                                                uT[:, j, o + c * TS:o + (c + 1) * TS], ident[:])
                last.then_inc(h_ready, 1)

            def router(g):
                pe.wait_ge(h_free, h_read_of("xnT2", g))
                hb = h_bank("router", g)
                for c in range(GT):
                    last = pe.matmul(hb[:, NE * c:NE * c + NE], xnT2[:, c * TS:(c + 1) * TS], rw[:],
                                     start=True, stop=True)
                last.then_inc(h_ready, 1)

            def router_T(g):
                pe.wait_ge(w9_done, g + 1)
                hb = h_bank("w9T", g)
                for c in range(GT):
                    last = pe.transpose(hb[0:NX, c * TS:(c + 1) * TS], w9[:, c, :], ident[:])
                last.then_inc(h_ready, 1)

            def hidden(g, e):
                for i in range(2):
                    hb = h_bank("hidden", g, e, i)
                    pe.matmul(hb[:], w1[:, e, i * 128:(i + 1) * 128], xnT2[:], start=True, stop=True)\
                        .then_inc(h_ready, 1)

            def expert_out(g, e):
                pe.wait_ge(h_free, h_read_of("hidden", g, e, 1))
                n = g * NX + e
                h = hh[n % 2]
                if n >= 2:
                    pe.wait_ge(acc, GT * (n - 1))
                yb = YY[n % 2]
                for c in range(GT):
                    for i in range(2):
                        last = pe.matmul(yb[:, c * TS:(c + 1) * TS], h[:, i, c * TS:(c + 1) * TS], w2[:, e, i, :],
                                         start=(i == 0), stop=(i == 1 and e != NE))
                    if e == NE:
                        last = pe.matmul(yb[:, c * TS:(c + 1) * TS], w9T[:, c * TS:(c + 1) * TS], b2[:],
                                         start=False, stop=True)
                last.then_inc(y_ready, 1)

            def proj(q):
                g, k = divmod(q, KP)
                c, h = divmod(k, NH)
                if q >= 2:
                    pe.wait_ge(sq_done, q - 1)
                b = BC[q % 2]
                xt = xnTs[g % 2][:, HALO + c * TS:HALO + (c + 1) * TS]
                for j in range(4):
                    col = COL_BC + h * 4 * NS + (0, 2, 1, 3)[j] * NS
                    last = pe.matmul(b[:, j * TS:(j + 1) * TS], winT[:, col:col + NS], xt, start=True, stop=True)
                last.then_inc(bc_ready, 1)

            def norms(q):
                h = q % NH
                tile = q // NH
                if q:
                    pe.wait_ge(vt_done, q)
                if h == 0 and tile:
                    pe.wait_ge(row_done, tile)
                pe.wait_ge(sq_done, q + 1)
                for i in range(2):
                    pe.matmul(VT[32 * h:32 * h + 1, 2 * TS:4 * TS], ones[:], sq[q % 2][:, 2 * i:2 * i + 2, :],
                              start=(i == 0), stop=(i == 1))

            def gv(q):
                v, w = vt[q % 2], wt[q % 8]
                pe.wait_ge(wv_done, q + 1)
                if q:
                    pe.wait_ge(gc_done, q)
                for i in range(2):
                    pe.matmul(GG[:, 0:TS], v[:, i, :], w[:, i, :], start=(i == 0), stop=(i == 1))
                for i in range(2):
                    last = pe.transpose(VT[:, TS * i:TS * (1 + i)], v[:, i, :], ident[:])
                last.then_inc(gv_done, 1)

            def norms_back(tile):
                pe.wait_ge(row_done, tile + 1)
                hb = h_bank("norms", tile)
                for i in range(2):
                    last = pe.transpose(hb[:, i * TS:(i + 1) * TS], rrow[:, i, :], ident[:])
                last.then_inc(h_ready, 1)

            def norms_C(tile):
                pe.wait_ge(inv_done, tile + 1)
                hb = h_bank("normsC", tile)
                for h in range(NH):
                    last = pe.matmul(hb[h % 2 * HD:(h % 2 + 1) * HD, h // 2 * TS:(h // 2 + 1) * TS],
                                     rinv[:, 1, h:h + 1].broadcast_to([128, HD]), ident[:], start=True, stop=True)
                last.then_inc(h_ready, 1)

            def tail(tile):
                pe.wait_ge(ub_done, tile + 1)
                pe.wait_ge(vt_done, NH * (tile + 1))
                if tile:
                    pe.wait_ge(z_done, tile)
                    pe.wait_ge(acc, GT * NX * (tile // GT))
                u = ub[tile % 2]
                head = lambda h: slice(h * HD, (h + 1) * HD)
                rows = lambda h: slice((h % 2) * HD, (h % 2 + 1) * HD)
                for h in range(NH):
                    last = pe.matmul(RR[rows(h), (h // 2) * 2 * NS:(h // 2 + 1) * 2 * NS], u[:, head(h)],
                                     vts[(NH * tile + h) % 8], start=True, stop=True)
                last.then_inc(r_done, 1)
                pe.wait_ge(gm_done, NH * (tile + 1))
                pe.wait_ge(xi_done, tile + 1)
                if tile:
                    pe.wait_ge(x2_done, tile)
                for h0 in range(0, NH, 2):
                    for j in range(3):
                        for h in (h0, h0 + 1):
                            q = NH * tile + h
                            o = OO[rows(h), (h // 2) * TS:(h // 2 + 1) * TS]
                            if j == 0:
                                pe.matmul(o, u[:, head(h)], gts[q % 8][:], start=True, stop=False)
                            else:
                                last = pe.matmul(o, xi[tile % 2][:, j - 1, head(h)], wt[q % 8][:, j - 1, :],
                                                 start=False, stop=(j == 2))
                last.then_inc(tail_done, 1)

            def tail_T(tile):
                pe.wait_ge(rts_done, tile + 1)
                for i in range(2):
                    for j in range(2):
                        last = pe.transpose(RR[:, i * DI + j * 128:i * DI + (j + 1) * 128], rts[:, j, i, :], ident[:])
                last.then_inc(rt_done, 1)

            def op(tile):
                pe.wait_ge(y3_done, tile + 1)
                for i in range(2):
                    last = pe.matmul(OO[:, 2 * TS:2 * TS + DM], y3[tile % 2][:, i, :], woT[:, i, :],
                                     start=(i == 0), stop=(i == 1))
                last.then_inc(op_done, 1)

            pe.wait_ge(cst_g, 1)
            pe.wait_ge(ld_u, LD_U)
            for k in range(MID_STEPS):
                front_early(0, k)
            pe.wait_ge(ld_w, LD_W)
            for i in range(2):
                for what in ("u", "z", "us"):
                    front_late(0, what, i)
            pe.wait_ge(ld_f, LD_F)
            for q in range(2):
                proj(q)
            for g in range(NG):
                for k in range(MID_STEPS):
                    for tile in due(g, k, OUT):
                        op(tile)
                    if 2 <= k + 1 < KP:
                        proj(KP * g + k + 1)
                    if g + 1 < NG and k in P_FIRST:
                        proj(KP * (g + 1) + P_FIRST.index(k))
                    for tile in due(g, k, NORMS):
                        norms_back(tile)
                    for tile in due(g, k, NORMS_C):
                        norms_C(tile)
                    for tile in due(g, k, TAIL):
                        tail(tile)
                    if 0 <= k - PRODUCTS < KP:
                        norms(KP * g + k - PRODUCTS)
                    for tile in due(g, k, TAIL_T):
                        tail_T(tile)
                    if 0 <= k - PRODUCTS < KP:
                        gv(KP * g + k - PRODUCTS)
                    if g + 1 < NG:
                        front_early(g + 1, k)
                        for what, at in (("u", L_U), ("z", L_Z), ("us", L_US)):
                            if k == at:
                                front_late(g + 1, what, 0)
                if g + 1 < NG:
                    front_late(g + 1, "u", 1)
                    front_late(g + 1, "z", 1)
                norm_T(LN2, g)
                router(g)
                if g + 1 < NG:
                    front_late(g + 1, "us", 1)
                for e in range(NX):
                    if e == NE:
                        router_T(g)
                    hidden(g, e)
                    if e:
                        expert_out(g, e - 1)
                expert_out(g, NE)

        @block.scalar
        def _(act):
            uses = [0]

            def h_read(*name):
                n = USE[name]
                assert n == uses[0]
                uses[0] += 1
                act.wait_ge(h_ready, n + 1)
                return HB[n % 2]

            by_tile = lambda t: t.rearrange("p (c t) -> p c t", c=GT)

            def front_early(g, k):
                if k == F_XNT:
                    hb = h_read("xnT", g)
                    xt = xnTs[g % 2]
                    if g:
                        act.wait_ge(h_free, h_read_of("xnT", g - 1))
                        act.activation(xt[:, 0:HALO], xnTs[(g - 1) % 2][:, GC:GC + HALO], ACT.Copy)
                    act.activation(xt[:, HALO:HALO + GC], hb[:], ACT.Copy).then_inc(h_free, 1)
                if k == F_LOGITS:
                    hb = h_read("logits", g)
                    act.activation(lraw[:], hb[:, 0:KP], ACT.Copy).then_inc(h_free, 1)
                if k == F_EXP:
                    act.wait_ge(dt_e, g + 1)
                    act.activation(le[:], lx[:], ACT.Exp).then_inc(dt_exp, 1)
                if k == F_ROWS:
                    hb = h_read("rows", g)
                    act.activation(dtr[:], hb[0:KP, 0:TS], ACT.Copy).then_inc(h_free, 1)
                if 0 <= k - F_BCAST < NH:
                    h = k - F_BCAST
                    hb = h_read("bcast", g, h)
                    if h == 0 and g:
                        act.wait_ge(de_done, g)
                        act.wait_ge(fill, FILL_OPS * g)
                        act.wait_ge(fill_d, 8 * g)
                    head = lambda t, o: view(t, o + h * SL, (NH * SL, GT), (1, TS))
                    act.activation(head(lden, 1), by_tile(hb[:]), ACT.Identity,
                                   bias=kvec[:, h:h + 1], scale=avec[:, h:h + 1])
                    act.activation(head(ab, DTN), by_tile(hb[:]), ACT.Copy).then_inc(h_free, 1)
                if k == F_LOG:
                    act.wait_ge(den_done, NH * (g + 1))
                    act.activation(lden[:], lden[:], ACT.Ln, bias=1.0).then_inc(ln_den, 1)

            def inverse_den(g):
                act.wait_ge(lcum, g + 1)
                if g:
                    act.wait_ge(wv_done, KP * g)
                act.activation(de[:, PC:2 * PC], lden[:], ACT.Exp, scale=-1.0).then_inc(inv_den, 1)

            def running_den(g):
                act.activation(de[:, 0:PC], lden[:], ACT.Exp).then_inc(de_done, 1)

            def front_late(g, what, i):
                hb = h_read(what, g, i)
                tiles = slice(i * 2 * TS, (i + 1) * 2 * TS)
                by_half = lambda t: t[:].rearrange("p (j t) -> p j t", j=2)
                before = GT * (g - 1) + 2 * (i + 1)
                if what == "u":
                    if g:
                        act.wait_ge(y3_done, before)
                    for j in range(2):
                        last = act.activation(uT[:, j, tiles], by_half(hb)[:, j, :], ACT.Silu, bias=biasu[:, j:j + 1])
                if what == "z":
                    if g:
                        act.wait_ge(gate_done, before)
                    last = act.activation(szT[:, :, tiles], by_half(hb), ACT.Silu)
                if what == "us":
                    if g:
                        act.wait_ge(ub_done, before)
                    last = act.activation(us[:, 2 * i:2 * i + 2, :], hb[:].rearrange("p (c d) -> p c d", c=2), ACT.Copy)
                last.then_inc(h_free, 1)

            def pair(q):
                act.wait_ge(bc_ready, q + 1)
                if q >= 2:
                    act.wait_ge(mul_done, q - 1)
                if q % KP == 0:
                    act.wait_ge(mat_p, q // KP + 1)
                    act.wait_ge(mat_e, 2 * (q // KP + 1))
                if q and q % KP == 0:
                    act.wait_ge(y_ready, NX * (q // KP))
                b = BC[q % 2]
                act.activation(yc[q % 2][:], b[:].rearrange("p (j t) -> p j t", j=4), ACT.Copy)\
                    .then_inc(yc_done, 1)
                if q >= 2:
                    act.wait_ge(gv_done, q - 1)
                act.activation(sq[q % 2], b[:].rearrange("p (j t) -> p j t", j=4), ACT.Square).then_inc(sq_done, 1)

            def g_copy(q):
                act.wait_ge(gv_done, q + 1)
                if q >= 8:
                    act.wait_ge(tail_done, (q - 8) // NH + 1)
                act.activation(gts[q % 8], GG[:, 0:TS], ACT.Copy).then_inc(gc_done, 1)

            def vt_copy(q):
                act.wait_ge(gv_done, q + 1)
                if q >= 8:
                    act.wait_ge(tail_done, (q - 8) // NH + 1)
                act.activation(vts[q % 8][:], VT[:, 0:2 * TS].rearrange("p (i n) -> p i n", i=2), ACT.Copy)\
                    .then_inc(vt_done, 1)
                if q % NH == NH - 1:
                    tile = q // NH
                    if tile:
                        act.wait_ge(h_free, h_read_of("norms", tile - 1))
                    act.activation(rrow[:], VT[:, 2 * TS:4 * TS].rearrange("p (j t) -> p j t", j=2), ACT.Copy)\
                        .then_inc(row_done, 1)

            def norms_copy(tile):
                hb = h_read("norms", tile)
                if tile:
                    act.wait_ge(inv_done, tile)
                act.activation(nsq[:], view(hb, 0, (TS, 2), (32, NH)), ACT.Identity, bias=eps_l2[:]).then_inc(h_free, 1)

            def norms_C_copy(tile):
                hb = h_read("normsC", tile)
                if tile:
                    act.wait_ge(gate_done, tile)
                act.activation(rcb[:], hb[:, 0:2 * TS].rearrange("p (i t) -> p i t", i=2), ACT.Copy)\
                    .then_inc(h_free, 1)

            def rts_copy(tile):
                act.wait_ge(r_done, tile + 1)
                if tile:
                    act.wait_ge(rt_done, tile)
                act.activation(rts[:], RR[:].rearrange("p (j i n) -> p j i n", j=2, i=2), ACT.Copy)\
                    .then_inc(rts_done, 1)

            def norm2(g):
                hb = h_read("xnT2", g)
                if g:
                    act.wait_ge(y_ready, NX * g)
                act.activation(xnT2[:], hb[:], ACT.Copy).then_inc(h_free, 1)

            def router_read(g):
                hb = h_read("router", g)
                act.activation(lg[:], hb[:, 0:GT * NE].rearrange("p (c e) -> p c e", c=GT), ACT.Copy)\
                    .then_inc(h_free, 1)

            def router_exp(g):
                act.wait_ge(lg_c, g + 1)
                act.activation(el[:], ls[:], ACT.Exp).then_inc(el_done, 1)

            def router_T(g):
                hb = h_read("w9T", g)
                act.activation(w9T[:], hb[0:NX, :], ACT.Copy).then_inc(h_free, 1)

            def gelus(g, e):
                n = g * NX + e
                for i in range(2):
                    hb = h_read("hidden", g, e, i)
                    if i == 0 and n >= 2:
                        act.wait_ge(y_ready, n - 1)
                    act.activation(hh[n % 2][:, i, :], hb[:], ACT.Gelu, bias=b1[:, e, i:i + 1]).then_inc(h_free, 1)

            act.wait_ge(ld_s, LD_S)
            act.activation(sgt[:, 2 * NH:4 * NH], sgt[:, 0:2 * NH], ACT.Exp, scale=-1.0).then_inc(prep_a, 1)
            act.wait_ge(cst_g, 1)
            act.wait_ge(prep, 1)
            for k in range(MID_STEPS):
                front_early(0, k)
            inverse_den(0)
            running_den(0)
            act.wait_ge(ld_w, LD_W)
            for i in range(2):
                for what in ("u", "z", "us"):
                    front_late(0, what, i)
            for g in range(NG):
                for k in range(MID_STEPS):
                    if k < KP:
                        pair(KP * g + k)
                    if 0 <= k - G_COPY < KP:
                        g_copy(KP * g + k - G_COPY)
                    for tile in due(g, k - 1, NORMS):
                        norms_copy(tile)
                    for tile in due(g, k - 1, NORMS_C):
                        norms_C_copy(tile)
                    for tile in due(g, k - 1, TAIL):
                        rts_copy(tile)
                    if g + 1 < NG:
                        front_early(g + 1, k - 1)
                        for what, at in (("u", L_U), ("z", L_Z), ("us", L_US)):
                            if k - 1 == at:
                                front_late(g + 1, what, 0)
                    if 0 <= k - PRODUCTS < KP:
                        vt_copy(KP * g + k - PRODUCTS)
                    if g + 1 < NG:
                        if k == F_INV:
                            inverse_den(g + 1)
                        if k == F_DEN:
                            running_den(g + 1)
                if g + 1 < NG:
                    front_late(g + 1, "u", 1)
                    front_late(g + 1, "z", 1)
                norm2(g)
                router_read(g)
                if g + 1 < NG:
                    front_late(g + 1, "us", 1)
                for e in range(NX):
                    if e == NE:
                        router_T(g)
                    gelus(g, e)
                    if e == 0:
                        router_exp(g)

        @block.vector
        def _(dve):
            chain = [0]

            def link(ins):
                chain[0] += 1
                ins.then_inc(dve_chain, 1)
                dve.wait_ge(dve_chain, chain[0])

            def norm_stats(kind, g):
                xg = xr[g % 3]
                if kind == LN1:
                    dve.wait_ge(ld_x[g], 16)
                for c in range(GT) if kind == LN1 else (GT - 1,):
                    last = dve.bn_stats(stats[:, c, :], xg[:, c, :])
                link(last)
                for c in range(GT):
                    last = dve.bn_aggr(mv[:, c, :], stats[:, c, :])
                link(last)
                dve.tensor_scalar(mv[:, :, 1], mv[:, :, 1], EPS_LN, None, ALU.add).then_inc(ln_var, 1)

            def norm_apply(kind, g):
                xg = xr[g % 3]
                n = ln_index(kind, g)
                dve.wait_ge(ln_rstd, n + 1)
                if kind == LN2:
                    last = ("xnT", g + 1) if g + 1 < NG else ("xnT2", g - 1)
                else:
                    last = ("xnT2", g - 2) if g >= 2 else ("xnT", g - 1)
                if n:
                    dve.wait_ge(h_ready, USE[last] + 1)
                for c in range(GT):
                    last = dve.tensor_scalar(xn[:, c, :], xg[:, c, :], mv[:, c, 0:1], rstd[:, c:c + 1],
                                             ALU.subtract, ALU.mult)
                last.then_inc(ln_xn, 1)

            def front_early(g, k):
                if k == F_STATS:
                    norm_stats(LN1, g)
                if k == F_XN:
                    norm_apply(LN1, g)
                if k == F_EXP:
                    dve.wait_ge(h_free, h_read_of("logits", g))
                    link(dve.tensor_tensor(lx[:].rearrange("p (c h) -> p c h", c=GT),
                                           lraw[:].rearrange("p (c h) -> p c h", c=GT),
                                           view(dtbb, 0, (0, GT), (1, NH)), ALU.add))
                    dve.tensor_scalar(lx[:], lx[:], 0.0, None, ALU.min).then_inc(dt_e, 1)
                if k == F_LOG1P:
                    dve.wait_ge(dt_exp, g + 1)
                    link(dve.tensor_scalar(le[:], le[:], E_MAX, None, ALU.min))
                    link(dve.tensor_scalar(lp[0][:], le[:], 1.0 / 9, None, ALU.mult))
                    for i, m in enumerate(range(8, 0, -1)):
                        c = (1.0 if m % 2 else -1.0) / m
                        link(dve.scalar_tensor_tensor(out=lp[(i + 1) % 2][:], in0=lp[i % 2][:], scalar=c, in1=le[:],
                                                      op0=ALU.add, op1=ALU.mult))
                    if g >= 2:
                        dve.wait_ge(ub_done, GT * (g - 1))
                    dve.tensor_scalar(dtts[g % 2][:], lp[0][:], DT_MIN, DT_MAX, ALU.max, ALU.min).then_inc(dt_done, 1)
                if k == F_BCAST and g:
                    dve.wait_ge(de_done, g)
                    dve.memset(view(lden, 0, (SL, KP), (1, 1)), 0.0)
                if 1 <= k - F_BCAST < 1 + NH:
                    h = k - F_BCAST - 1
                    dve.wait_ge(h_free, h_read_of("bcast", g, h))
                    head = lambda t, o: view(t, o + h * SL, (NH * SL, GT), (1, TS))
                    dve.tensor_tensor(head(lden, 1), head(lden, 1), head(ab, DTN), ALU.mult).then_inc(den_done, 1)
                if 0 <= k - F_SCAN < F_CENTRE - F_SCAN:
                    dve.wait_ge(ln_den, g + 1)
                    n = KP // (F_CENTRE - F_SCAN)
                    for j in range((k - F_SCAN) * n, (k - F_SCAN + 1) * n):
                        last = dve.tensor_tensor_scan(ab[:, LCS + j * SL:LCS + (j + 1) * SL],
                                                      ones[:].broadcast_to([128, SL]), lden[:, j * SL:(j + 1) * SL],
                                                      0.0, ALU.mult, ALU.add)
                    if k == F_CENTRE - 1:
                        last.then_inc(scan_done, 1)
                if k == F_CENTRE:
                    dve.wait_ge(scan_done, g + 1)
                    dve.tensor_tensor(view(lden, 0, (SL, KP), (1, SL)), view(ab, LCS, (SL, KP), (1, SL)),
                                      view(ab, LCS + MID, (SL, KP), (0, SL)), ALU.subtract).then_inc(lcum, 1)

            def beta(g):
                dve.wait_ge(inv_den, g + 1)
                dve.tensor_tensor(view(ab, PC + 1, (SL, KP), (1, TS)), view(de, PC + 1, (SL, KP), (1, TS)),
                                  view(ab, DTN, (SL, KP), (1, TS)), ALU.mult).then_inc(beta_done, 1)

            def alpha(g):
                dve.wait_ge(beta_done, g + 1)
                dve.wait_ge(de_done, g + 1)
                for h in range(NH):
                    last = dve.scalar_tensor_tensor(out=view(ab, h * SL + 1, (NH * SL, GT), (1, TS)),
                                                    in0=view(de, h * SL, (NH * SL, GT), (1, TS)),
                                                    scalar=avec[:, h:h + 1],
                                                    in1=view(ab, DTN + h * SL, (NH * SL, GT), (1, TS)),
                                                    op0=ALU.mult, op1=ALU.mult)
                last.then_inc(ab_done, 1)

            Y0, W0 = 0, 2 * PC
            issued = [0]

            def step_op(*args):
                dve.wait_ge(step, issued[0] - 1)
                dve.tensor_tensor(*args).then_inc(step, 1)
                issued[0] += 1

            def step_start(g):
                if g:
                    dve.wait_ge(wv_done, KP * g)
                dve.memset(view(pr, MID, (3 * PC, 2), (SL, KP)), 1.0)
                dve.memset(view(pr, PC + MID, (PC, 2), (SL, KP)), 0.0).then_inc(step, 1)
                issued[0] += 1
                dve.wait_ge(step, issued[0])

            def matrices(g, part):
                def after(n):
                    dve.wait_ge(mat_d, MAT_OPS * g + n)

                if part == 0:
                    dve.wait_ge(ab_done, g + 1)
                    if g:
                        dve.wait_ge(wv_done, KP * g)
                    for f in range(2):
                        dve.tensor_tensor(scr(f, 0), c1(f, 0), c2(f, 0), ALU.mult).then_inc(mat_d, 1)
                    dve.tensor_tensor(scr_x(1), c1(1, 1), c2(1, 0), ALU.mult).then_inc(mat_d, 1)
                if part == 1:
                    for f in range(2):
                        after(1 + f)
                        dve.tensor_scalar(scr(f, 1), scr(f, 0), -1.0, 1.0, ALU.mult, ALU.add).then_inc(mat_d, 1)
                    after(3)
                    dve.tensor_scalar(entry(1, "x", "x"), scr_x(1), -1.0, 1.0, ALU.mult, ALU.add).then_inc(mat_d, 1)
                    for f in range(2):
                        after(4 + f)
                        dve.tensor_tensor(scr(f, 0), c1(f, 1), scr(f, 1), ALU.mult).then_inc(mat_d, 1)
                    after(6)
                    dve.tensor_tensor(scr_x(1), c2(1, 1), entry(1, "x", "x"), ALU.mult).then_inc(mat_d, 1)
                if part == 2:
                    for f in range(2):
                        after(7 + f)
                        dve.scalar_tensor_tensor(out=entry(f, "x", "v"), in0=scr(f, 0), scalar=-1.0, in1=c1(f, 0),
                                                 op0=ALU.mult, op1=ALU.subtract).then_inc(mat_d, 1)
                    after(9)
                    dve.tensor_tensor(entry(1, "v", "x"), c2(1, 0), scr_x(1), ALU.add).then_inc(mat_d, 1)
                    for f in range(2):
                        after(10 + f)
                        dve.tensor_tensor(scr(f, 0), c2(f, 1), entry(f, "x", "v"), ALU.mult).then_inc(mat_d, 1)
                    for f in range(2):
                        after(13 + f)
                        dve.tensor_tensor(entry(f, "v", "v"), scr(f, 1), scr(f, 0), ALU.add).then_inc(mat_e, 1)
                    after(MAT_OPS)
                    dve.wait_ge(mat_e, 2 * (g + 1))
                    dve.wait_ge(mat_p, g + 1)

            def step_products(i):
                for f in range(2):
                    slot = MID + (2 * i if f else -2 * i)
                    step_op(view(tp[f], 0, (4 * KP, 2), (2 * KP, 2), (1, 2 * KP)),
                            view(big, 4 * f * DS * KP + i * KP, (DS * KP, 4), (0, 2), (1, KP)),
                            view(pr, slot, (W0, 2), (0, 2), (SL, 2 * KP)), ALU.mult)

            def step_sums(i):
                for f in range(2):
                    slot = MID + (2 * i + 2 if f else -2 * i - 2)
                    step_op(view(pr, slot, (W0, 2), (SL, 2 * KP)),
                            view(tp[f], 0, (2 * KP, 2), (1, 2 * KP)),
                            view(tp[f], 4 * KP, (2 * KP, 2), (1, 2 * KP)), ALU.add)

            filled = [0]

            def fill_op(*args):
                if filled[0] >= 2:
                    dve.wait_ge(fill_d, filled[0] - 1)
                dve.tensor_tensor(*args).then_inc(fill_d, 1)
                filled[0] += 1

            def pair(q):
                o = (q % KP) * SL
                dve.wait_ge(yc_done, q + 1)
                y = yc[q % 2]
                dve.tensor_tensor(y[:, 2:4, :], y[:, 2:4, :], view(de, o, (PC + 1, 2), (1, TS)), ALU.mult)\
                    .then_inc(vc_done, 1)

            def products(q):
                o = (q % KP) * SL
                if q >= 2:
                    dve.wait_ge(wv_done, q - 1)
                dve.wait_ge(vc_done, q + 1)
                m, y = mm[q % 2], yc[q % 2]
                dve.tensor_tensor(m[:, 0:2], view(y, TS, (TS, 2), (0, 2), (1, TS)),
                                  view(pr, o + 1, (-1, 2), (PC, 2), (1, TS)), ALU.mult)
                dve.tensor_tensor(m[:, 2:4], view(y, 0, (3 * TS, 2), (0, 2), (1, TS)),
                                  view(pr, W0 + o + 1, (0, 2), (PC, 2), (1, TS)), ALU.mult).then_inc(mul_done, 1)

            def state_sum(tile):
                dve.wait_ge(rt_done, tile + 1)
                if tile:
                    dve.wait_ge(xi_done, tile + 1)
                dve.tensor_tensor(zz[:], xi[tile % 2][:], RR[:].rearrange("p (i d) -> p i d", i=2), ALU.add)\
                    .then_inc(z_done, 1)

            def state(tile):
                k = NH * (tile % GT)
                dve.wait_ge(tr_done, tile // GT + 1)
                dve.wait_ge(z_done, tile)
                pick = lambda col: view(tr, col * 2 * KP + k, (KP, 2), (1, NH), (0, HD))
                full = lambda t: t[:].rearrange("p i (h d) -> p i h d", h=NH)
                dve.tensor_tensor(full(x1), pick(0), view(zz, 0, (0, 2), (HD, NH), (1, HD)), ALU.mult)
                dve.tensor_tensor(full(x2), pick(1), view(zz, DI, (0, 2), (HD, NH), (1, HD)), ALU.mult)\
                    .then_inc(x_done, 1)
                dve.wait_ge(x_done, tile)
                dve.tensor_tensor(xi[tile % 2][:], x1[:], x2[:], ALU.add).then_inc(xi_done, 1)

            def tile_out(tile):
                dve.wait_ge(tail_done, tile + 1)
                dve.wait_ge(gate_done, tile + 1)
                if tile >= 2:
                    dve.wait_ge(y3_done, tile - 1)
                dve.tensor_tensor(y1[tile % 2][:], OO[:, 0:2 * TS].rearrange("p (i t) -> p i t", i=2),
                                  gate[tile % 2][:], ALU.mult).then_inc(y1_done, 1)

            def add_skip(tile):
                g, c = divmod(tile, GT)
                dve.wait_ge(y1_done, tile + 1)
                dve.wait_ge(skip_done, g + 1)
                if tile >= 2:
                    dve.wait_ge(op_done, tile - 1)
                dve.tensor_tensor(y3[tile % 2][:], y1[tile % 2][:], uT[:, :, c * TS:(c + 1) * TS], ALU.add)\
                    .then_inc(y3_done, 1)

            def residual(tile):
                dve.wait_ge(op_done, tile + 1)
                xg = xr[(tile // GT) % 3][:, tile % GT, :]
                dve.tensor_tensor(xg, OO[:, 2 * TS:2 * TS + DM], xg, ALU.add).then_inc(x2_done, 1)
                c = tile % GT
                if c:
                    dve.wait_ge(x2_done, tile)
                    dve.bn_stats(stats[:, c - 1, :], xr[(tile // GT) % 3][:, c - 1, :])

            def router_max(g):
                dve.wait_ge(h_free, h_read_of("router", g))
                link(dve.tensor_tensor(lg[:], lg[:], view(rb, 0, (0, GT), (1, NE)), ALU.add))
                link(dve.tensor_reduce(lm[:], lg[:], AX.X, ALU.max))
                dve.tensor_tensor(ls[:], lg[:], view(lm, 0, (1, GT), (0, NE)), ALU.subtract).then_inc(lg_c, 1)

            def router_stage(g, stage):
                if stage:
                    dve.wait_ge(router_d, (ROUTER_STAGES - 1) * g + stage)
                lj = view(lg, 0, (NE, GT), (0, NE), (1, NE))
                li = view(lg, 0, (NE, GT), (1, NE), (0, NE))
                flat = lambda t: t.rearrange("p c e j -> p c (e j)")
                if stage == 0:
                    dve.tensor_tensor(cmp, lj, li, ALU.is_gt)
                    dve.tensor_tensor(tie, lj, li, ALU.is_equal).then_inc(router_d, 1)
                if stage == 1:
                    dve.tensor_tensor(flat(tie), flat(tie), view(before, 0, (0, GT), (1, NE * NE)), ALU.mult)\
                        .then_inc(router_d, 1)
                if stage == 2:
                    dve.tensor_tensor(cmp, cmp, tie, ALU.add).then_inc(router_d, 1)
                if stage == 3:
                    dve.tensor_reduce(rank[:], cmp, AX.X, ALU.add).then_inc(router_d, 1)
                if stage == 4:
                    dve.wait_ge(el_done, g + 1)
                    dve.tensor_reduce(esum[:], el[:], AX.X, ALU.add).then_inc(router_d, 1)
                if stage == 5:
                    dve.reciprocal(einv[:], esum[:]).then_inc(router_d, 1)
                if stage == 6:
                    dve.scalar_tensor_tensor(out=selw[:], in0=rank[:], scalar=1.5, in1=el[:],
                                             op0=ALU.is_lt, op1=ALU.mult).then_inc(router_d, 1)
                if stage == 7:
                    if g:
                        dve.wait_ge(acc, GT * NX * g)
                    dve.memset(w9[:, :, NE:NX], 1.0)
                    dve.tensor_tensor(w9[:, :, 0:NE], selw[:], view(einv, 0, (1, GT), (0, NE)), ALU.mult)\
                        .then_inc(w9_done, 1)

            def add_expert(g, e):
                n = g * NX + e
                dve.wait_ge(y_ready, n + 1)
                if e == 0:
                    dve.wait_ge(w9_done, g + 1)
                yb = YY[n % 2]
                for c in range(GT):
                    if e:
                        dve.wait_ge(acc, GT * (n - 1) + c + 1)
                    xg = xr[g % 3][:, c, :]
                    dve.scalar_tensor_tensor(out=xg, in0=yb[:, c * TS:(c + 1) * TS], scalar=w9[:, c, e:e + 1],
                                             in1=xg, op0=ALU.mult, op1=ALU.add).then_inc(acc, 1)

            dve.memset(ones[:], 1.0)
            dve.memset(mhalf[:], -0.5)
            dve.memset(eps_l2[:], EPS_L2)
            dve.memset(xnTs[0][:, 0:HALO], 0.0)
            dve.memset(VT[:], 1.0)
            dve.memset(view(lden, 0, (SL, KP), (1, 1)), 0.0).then_inc(cst, 1)
            dve.wait_ge(cst, 1)
            front_early(0, F_STATS)
            dve.wait_ge(prep_a, 1)
            link(dve.tensor_scalar(sgt[:, 2 * NH:], sgt[:, 2 * NH:], 1.0, None, ALU.add))
            link(dve.reciprocal(sgt[:, 2 * NH:], sgt[:, 2 * NH:]))
            dve.tensor_scalar(kvec[:], sgt[:, 3 * NH:], K_MAX, None, ALU.mult)
            link(dve.tensor_scalar(theta[:], sgt[:, 2 * NH:3 * NH], PI, None, ALU.mult))
            dve.tensor_tensor(avec[:], theta[:], theta[:], ALU.mult).then_inc(prep, 1)
            dve.wait_ge(prep, 1)
            front_early(0, F_XN)
            dve.wait_ge(ld_u, LD_U)
            for k in range(TAPS):
                last = dve.tensor_tensor(taps[:, k, :], taps[:, k, :], winT[:, COL_U:COL_U + DI], ALU.mult)
            last.then_inc(taps_done, 1)
            for k in range(F_XNT, MID_STEPS):
                front_early(0, k)
            beta(0)
            alpha(0)
            for part in range(3):
                matrices(0, part)
            for g in range(NG):
                step_start(g)
                for i in range(DS):
                    step_products(i)
                    if g and 2 * i < ROUTER_STAGES:
                        router_stage(g - 1, 2 * i)
                    step_sums(i)
                    if g and 2 * i + 1 < ROUTER_STAGES:
                        router_stage(g - 1, 2 * i + 1)
                    e, late = divmod(i - EXPERT_FIRST, EXPERT_EVERY)
                    if g and late == 0 and 0 <= e < NX:
                        add_expert(g - 1, e)
                dve.wait_ge(step, STEP_OPS * (g + 1))
                fill_slots(fill_op, mm, DS - FILL_LAST, FILL_LAST)
                dve.wait_ge(fill, FILL_OPS * (g + 1))
                dve.wait_ge(fill_d, 8 * (g + 1))
                for k in range(MID_STEPS):
                    for tile in due(g, k, STATE_SUM):
                        if tile % GT < GT - 1:
                            state_sum(tile)
                    if k < KP:
                        pair(KP * g + k)
                    for tile in due(g, k, OUT):
                        residual(tile)
                    for tile in due(g, k, TILE_OUT):
                        tile_out(tile)
                    if k < KP:
                        products(KP * g + k)
                    for tile in due(g, k, STATE):
                        if tile:
                            state(tile)
                    for tile in due(g, k, TILE_OUT):
                        add_skip(tile)
                    if g + 1 < NG:
                        front_early(g + 1, k)
                        if k == F_BETA:
                            beta(g + 1)
                        if k == F_ALPHA:
                            alpha(g + 1)
                dve.wait_ge(x2_done, GT * (g + 1))
                norm_stats(LN2, g)
                if g + 1 < NG:
                    state_sum(GT * (g + 1) - 1)
                    matrices(g + 1, 0)
                norm_apply(LN2, g)
                if g + 1 < NG:
                    matrices(g + 1, 1)
                router_max(g)
                if g + 1 < NG:
                    matrices(g + 1, 2)
            for stage in range(ROUTER_STAGES):
                router_stage(NG - 1, stage)
            for e in range(NX):
                add_expert(NG - 1, e)

        @block.gpsimd
        def _(pool):
            chain = [0]

            def link(ins):
                chain[0] += 1
                ins.then_inc(pool_chain, 1)
                pool.wait_ge(pool_chain, chain[0])

            def rstd_of(n):
                pool.wait_ge(ln_var, n + 1)
                if n:
                    pool.wait_ge(ln_xn, n)
                pool.tensor_tensor(rstd[:], mv[:, :, 1], mhalf[:, 0:GT], ALU.pow).then_inc(ln_rstd, 1)

            def crossings(g):
                p, d = pr, de
                W0 = 2 * PC
                if g:
                    link(pool.tensor_copy(edge[:, :, 0:NH], edge[:, :, KP:KP + NH]))
                pool.tensor_copy(edge[:, 0:2, NH:], view(p, TS, (PC, 2), (SL, KP)))
                link(pool.tensor_tensor(edge[:, 2:4, NH:], view(p, W0 + TS, (PC, 2), (SL, KP)),
                                        view(d, PC + TS, (0, 2), (SL, KP)), ALU.mult))
                link(pool.tensor_tensor(ew[:], edge[:, 2:4, 0:KP], view(d, 0, (0, 2), (SL, KP)), ALU.mult))
                first = lambda o: view(p, o, (0, 2), (SL, KP))
                y = edge[:, 0:2, 0:KP]
                pool.tensor_tensor(tra[:, 0], first(W0 + PC), y, ALU.mult)
                pool.tensor_tensor(tra[:, 1], first(PC), ew[:], ALU.mult)
                pool.tensor_tensor(tra[:, 2], first(0), ew[:], ALU.mult)
                link(pool.tensor_tensor(tra[:, 3], first(W0), y, ALU.mult))
                pool.tensor_tensor(tr[:, :, 0, :], tra[:, 0], tra[:, 1], ALU.subtract)
                pool.tensor_tensor(tr[:, :, 1, :], tra[:, 2], tra[:, 3], ALU.subtract).then_inc(tr_done, 1)

            def wv(q):
                pool.wait_ge(mul_done, q + 1)
                if q >= 8:
                    pool.wait_ge(tail_done, (q - 8) // NH + 1)
                m = mm[q % 2]
                pool.tensor_tensor(wt[q % 8][:], m[:, 0], m[:, 3], ALU.add)
                if q >= 2:
                    pool.wait_ge(gv_done, q - 1)
                pool.tensor_tensor(vt[q % 2][:, 0, :], m[:, 2, 1, :], m[:, 1, 1, :], ALU.subtract)
                pool.tensor_tensor(vt[q % 2][:, 1, :], m[:, 1, 0, :], m[:, 2, 0, :], ALU.subtract).then_inc(wv_done, 1)

            def matrices(g):
                pool.wait_ge(ab_done, g + 1)
                link(pool.tensor_tensor(scr_x(0), c1(0, 1), c2(0, 0), ALU.mult))
                link(pool.tensor_scalar(entry(0, "x", "x"), scr_x(0), -1.0, 1.0, ALU.mult, ALU.add))
                link(pool.tensor_tensor(scr_x(0), c2(0, 1), entry(0, "x", "x"), ALU.mult))
                pool.tensor_tensor(entry(0, "v", "x"), c2(0, 0), scr_x(0), ALU.add).then_inc(mat_p, 1)

            def mask(q):
                pool.wait_ge(gc_done, q + 1)
                pool.affine_select(out=gts[q % 8], in_=gts[q % 8], compare_op=ALU.is_ge, fill=0.0, base=0,
                                   pattern=[[1, TS]], channel_multiplier=-1).then_inc(gm_done, 1)

            def skip_gate(g):
                if g == 0:
                    pool.wait_ge(ld_w, LD_W)
                pool.wait_ge(h_free, h_read_of("us", g, 1))
                for i in range(2):
                    last = pool.tensor_scalar(uT[:, i, :], uT[:, i, :], skipT[:, i:i + 1], None, ALU.mult)
                link(last)
                pool.tensor_tensor(uT[:], uT[:], szT[:], ALU.mult).then_inc(skip_done, 1)

            filled = [0]

            def fill_op(*args):
                if filled[0] >= 2:
                    pool.wait_ge(fill, filled[0] - 1)
                pool.tensor_tensor(*args).then_inc(fill, 1)
                filled[0] += 1

            def ubar(tile):
                g, c = divmod(tile, GT)
                pool.wait_ge(h_free, h_read_of("norms", tile))
                pool.tensor_tensor(rinv[:].rearrange("p i h -> p (i h)"), nsq[:].rearrange("p i h -> p (i h)"),
                                   mhalf[:], ALU.pow).then_inc(inv_done, 1)
                pool.wait_ge(inv_done, tile + 1)
                link(pool.tensor_tensor(du[:], rinv[:, 0, :], dtts[g % 2][:, NH * c:NH * c + NH], ALU.mult))
                if tile >= 2:
                    pool.wait_ge(tail_done, tile - 1)
                pool.tensor_tensor(ub[tile % 2][:].rearrange("p (h d) -> p h d", h=NH),
                                   us[:, c, :].rearrange("p (h d) -> p h d", h=NH),
                                   view(du, 0, (1, NH), (0, HD)), ALU.mult).then_inc(ub_done, 1)

            def gates(tile):
                c = tile % GT
                pool.wait_ge(h_free, h_read_of("normsC", tile))
                if tile >= 2:
                    pool.wait_ge(y1_done, tile - 1)
                pool.tensor_tensor(gate[tile % 2][:], rcb[:], szT[:, :, c * TS:(c + 1) * TS], ALU.mult)\
                    .then_inc(gate_done, 1)

            pool.memset(xi[0][:], 0.0).then_inc(xi_done, 1)
            pool.memset(edge[:], 0.0)
            pool.memset(ident[:], 0.0)
            link(pool.memset(before[:], 1.0))
            pool.affine_select(out=ident[:], in_=ident[:], compare_op=ALU.not_equal, fill=1.0, base=0,
                               pattern=[[-1, 128]], channel_multiplier=1)
            link(pool.affine_select(out=before[:], in_=before[:], compare_op=ALU.is_gt, fill=0.0, base=0,
                                    pattern=[[1, NE], [-1, NE]], channel_multiplier=0))
            pool.wait_ge(cst, 1)
            pool.memset(ew[:], 0.0).then_inc(cst_g, 1)
            rstd_of(0)
            matrices(0)
            for g in range(NG):
                skip_gate(g)
                i0 = 0
                for n in FILLS:
                    pool.wait_ge(step, STEP_OPS * g + 1 + 4 * (i0 + n - 1))
                    fill_slots(fill_op, tf, i0, n)
                    i0 += n
                for k in range(MID_STEPS):
                    for tile in due(g, k, UBAR):
                        ubar(tile)
                    for tile in due(g, k, GATES):
                        gates(tile)
                    if k == 1:
                        crossings(g)
                    if 0 <= k - MASK < KP:
                        mask(KP * g + k - MASK)
                    if k < KP:
                        wv(KP * g + k)
                    if g + 1 < NG and k == F_STATS:
                        rstd_of(ln_index(LN1, g + 1))
                if g + 1 < NG:
                    matrices(g + 1)
                rstd_of(ln_index(LN2, g))


def kernel(**inputs):
    import numpy as np
    import concourse.bacc as bacc
    from concourse.bass_utils import run_bass_kernel_spmd

    a = {n.split("_", 1)[1]: np.asarray(v) for n, v in inputs.items()}
    hidden_cols = lambda v: v.reshape(-1, 2, 128).transpose(2, 0, 1)
    laid = {
        "x": a["attn_x"], "w_inT": a["attn_W_in"].T, "dw_wT": a["attn_dw_weight"].T,
        "dw_bT": a["attn_dw_bias"].reshape(2, 128).T,
        "w_outT": a["attn_W_out"].T, "skipT_in": a["attn_skip"].reshape(2, 128).T, "dt_bias": a["attn_dt_bias"],
        "theta_rawT": a["attn_theta_raw"].T, "k_rawT": a["attn_k_raw"].T,
        "router_w": a["ffn_router_w"], "router_b": a["ffn_router_b"],
        "sw1": a["ffn_sw1"], "sb1T": hidden_cols(a["ffn_sb1"])[:, 0], "sw2": a["ffn_sw2"], "sb2": a["ffn_sb2"],
        "rw1": a["ffn_rw1"], "rb1T": hidden_cols(a["ffn_rb1"]), "rw2": a["ffn_rw2"], "rb2": a["ffn_rb2"],
    }
    nc = bacc.Bacc("TRN2", target_bir_lowering=False, num_devices=1)
    arrays, args = {}, {}
    for name, v in laid.items():
        v = np.ascontiguousarray(v)
        arrays[f"in_{name}"] = v
        args[name] = nc.dram_tensor(f"in_{name}", v.shape, mybir.dt.from_np(v.dtype), kind="ExternalInput").ap()
    args["out"] = nc.dram_tensor("out_0", (1, T, DM), F32, kind="ExternalOutput").ap()
    build(nc, **args)
    r = run_bass_kernel_spmd(nc, [arrays], core_ids=[0])
    return r.results[0]["out_0"]
```
